# Optimizing a Trainium2 kernel written in Bass

```python
import numpy as np
import jax
import jax.numpy as jnp

def _softmax(x, axis=-1):
    return jax.nn.softmax(x, axis=axis)

def _gelu(x):
    return jax.nn.gelu(x, approximate=True)

def _silu(x):
    return jax.nn.silu(x)

def _sigmoid(x):
    return jax.nn.sigmoid(x)

def _layernorm(x, axis=-1, eps=1e-05):
    m = jnp.mean(x, axis=axis, keepdims=True)
    v = jnp.var(x, axis=axis, keepdims=True)
    return (x - m) / jnp.sqrt(v + eps)

def _scatter_add(tgt, idx, src, axis=0):
    return tgt.at[idx].add(src)

def _segment_sum(src, seg, n):
    return jax.ops.segment_sum(src, seg, n)
kernel_name = 'mk_conv_seq_d2_conv_nchw256_r4_748b8f'

def setup_inputs(seed: int=0):
    np.random.seed(seed)
    _w = jnp.asarray

    def _rec_inputs():
        import jax
        import jax.numpy as jnp
        _gk = jax.random.key(seed)
        x = -0.0003929 + 0.9999 * jax.random.normal(jax.random.fold_in(_gk, 1), (4, 64, 32, 32), jnp.float32)
        return x
    x = _rec_inputs()

    def _L0_conv_setup():
        import jax, jax.numpy as jnp
        import numpy as np
        HEADS, LEVELS, POINTS = (8, 1, 4)
        key = jax.random.key(seed)
        ks = jax.random.split(key, 6)
        B, C, H, W = (4, 64, 32, 32)
        s = 0.02
        return {'x': jax.random.normal(ks[0], (B, C, H, W), jnp.float32), 'W_value': jax.random.normal(ks[1], (C, C), jnp.float32) * s, 'b_value': jnp.zeros((C,), jnp.float32), 'W_off': jax.random.normal(ks[2], (C, HEADS * LEVELS * POINTS * 2), jnp.float32) * s, 'b_off': jnp.zeros((HEADS * LEVELS * POINTS * 2,), jnp.float32), 'W_attn': jax.random.normal(ks[3], (C, HEADS * LEVELS * POINTS), jnp.float32) * s, 'b_attn': jnp.zeros((HEADS * LEVELS * POINTS,), jnp.float32), 'W_out': jax.random.normal(ks[4], (C, C), jnp.float32) * s, 'b_out': jnp.zeros((C,), jnp.float32)}
    _L0_conv_all = _L0_conv_setup()
    _L0_conv_in = {k: v for k, v in _L0_conv_all.items() if k in ('W_value', 'b_value', 'W_off', 'b_off', 'W_attn', 'b_attn', 'W_out', 'b_out')}
    del _L0_conv_all

    def _L1_conv_setup():
        import jax, jax.numpy as jnp
        import numpy as np
        from jax import lax
        N, C, H, W = (32, 64, 56, 56)
        K = 3
        BN_EPS = 1e-05

        def _binary_activation(x):
            sq = x * x
            o1 = jnp.where(x < -1.0, -1.0, sq + 2.0 * x)
            o2 = jnp.where(x < 0.0, o1, -sq + 2.0 * x)
            o3 = jnp.where(x < 1.0, o2, 1.0)
            return lax.stop_gradient(jnp.sign(x) - o3) + o3

        def _binarize_weights(w):
            scale = lax.stop_gradient(jnp.mean(jnp.abs(w), axis=(1, 2, 3), keepdims=True))
            cw = jnp.clip(w, -1.0, 1.0)
            return lax.stop_gradient(scale * jnp.sign(w) - cw) + cw
        key = jax.random.key(seed)
        ks = jax.random.split(key, 3)
        x = jax.random.normal(ks[0], (N, C, H, W), dtype=jnp.float32)
        conv_w = jax.random.uniform(ks[1], (C, C, K, K), dtype=jnp.float32) * 0.001
        return {'x': x, 'move0_bias': jnp.zeros((1, C, 1, 1), jnp.float32), 'conv_w': conv_w, 'bn_gamma': jnp.ones((C,), jnp.float32), 'bn_beta': jnp.zeros((C,), jnp.float32), 'move1_bias': jnp.zeros((1, C, 1, 1), jnp.float32), 'prelu_a': jnp.full((C,), 0.25, jnp.float32), 'move2_bias': jnp.zeros((1, C, 1, 1), jnp.float32)}
    _L1_conv_all = _L1_conv_setup()
    _L1_conv_in = {k: v for k, v in _L1_conv_all.items() if k in ('move0_bias', 'conv_w', 'bn_gamma', 'bn_beta', 'move1_bias', 'prelu_a', 'move2_bias')}
    del _L1_conv_all
    return {'x': x, 'L0_conv_W_value': _L0_conv_in['W_value'], 'L0_conv_b_value': _L0_conv_in['b_value'], 'L0_conv_W_off': _L0_conv_in['W_off'], 'L0_conv_b_off': _L0_conv_in['b_off'], 'L0_conv_W_attn': _L0_conv_in['W_attn'], 'L0_conv_b_attn': _L0_conv_in['b_attn'], 'L0_conv_W_out': _L0_conv_in['W_out'], 'L0_conv_b_out': _L0_conv_in['b_out'], 'L1_conv_move0_bias': _L1_conv_in['move0_bias'], 'L1_conv_conv_w': _L1_conv_in['conv_w'], 'L1_conv_bn_gamma': _L1_conv_in['bn_gamma'], 'L1_conv_bn_beta': _L1_conv_in['bn_beta'], 'L1_conv_move1_bias': _L1_conv_in['move1_bias'], 'L1_conv_prelu_a': _L1_conv_in['prelu_a'], 'L1_conv_move2_bias': _L1_conv_in['move2_bias']}

def reference(x, L0_conv_W_value, L0_conv_b_value, L0_conv_W_off, L0_conv_b_off, L0_conv_W_attn, L0_conv_b_attn, L0_conv_W_out, L0_conv_b_out, L1_conv_move0_bias, L1_conv_conv_w, L1_conv_bn_gamma, L1_conv_bn_beta, L1_conv_move1_bias, L1_conv_prelu_a, L1_conv_move2_bias):
    import jax
    import jax.numpy as jnp

    def _L0_conv_ref(x, W_value, b_value, W_off, b_off, W_attn, b_attn, W_out, b_out):
        import jax, jax.numpy as jnp
        import numpy as np
        HEADS, LEVELS, POINTS = (8, 1, 4)
        B, C, H, W = x.shape
        d = C // HEADS
        Nq = H * W
        q = x.reshape(B, C, Nq).transpose(0, 2, 1)
        v = (q @ W_value + b_value).reshape(B, Nq, HEADS, d)
        vflat = v.transpose(0, 2, 3, 1)
        off = (q @ W_off + b_off).reshape(B, Nq, HEADS, LEVELS, POINTS, 2)
        attn = jax.nn.softmax((q @ W_attn + b_attn).reshape(B, Nq, HEADS, LEVELS * POINTS), axis=-1)
        attn = attn.reshape(B, Nq, HEADS, POINTS)
        gy, gx = jnp.meshgrid(jnp.linspace(0.0, 1.0, H), jnp.linspace(0.0, 1.0, W), indexing='ij')
        ref = jnp.stack((gx, gy), axis=-1).reshape(1, Nq, 1, 1, 2)
        norm = jnp.array([W, H], jnp.float32)
        loc = ref + off[:, :, :, 0, :, :] / norm
        ix = loc[..., 0] * W - 0.5
        iy = loc[..., 1] * H - 0.5
        x0f, y0f = (jnp.floor(ix), jnp.floor(iy))
        wx1, wy1 = (ix - x0f, iy - y0f)
        x0, y0 = (x0f.astype(jnp.int32), y0f.astype(jnp.int32))

        def gather(xi, yi):
            valid = ((xi >= 0) & (xi < W) & (yi >= 0) & (yi < H)).astype(jnp.float32)
            idx = jnp.clip(yi, 0, H - 1) * W + jnp.clip(xi, 0, W - 1)
            idx = idx.transpose(0, 2, 1, 3).reshape(B, HEADS, 1, Nq * POINTS)
            g = jnp.take_along_axis(vflat, idx, axis=3)
            m = valid.transpose(0, 2, 1, 3).reshape(B, HEADS, 1, Nq * POINTS)
            return g * m

        def wshape(w):
            return w.transpose(0, 2, 1, 3).reshape(B, HEADS, 1, Nq * POINTS)
        sampled = gather(x0, y0) * wshape((1 - wx1) * (1 - wy1)) + gather(x0 + 1, y0) * wshape(wx1 * (1 - wy1)) + gather(x0, y0 + 1) * wshape((1 - wx1) * wy1) + gather(x0 + 1, y0 + 1) * wshape(wx1 * wy1)
        aw = attn.transpose(0, 2, 1, 3).reshape(B, HEADS, 1, Nq, POINTS)
        out = (sampled.reshape(B, HEADS, d, Nq, POINTS) * aw).sum(-1)
        out = out.transpose(0, 3, 1, 2).reshape(B, Nq, C)
        out = out @ W_out + b_out + q
        return out.transpose(0, 2, 1).reshape(B, C, H, W)

    def _L1_conv_ref(x, move0_bias, conv_w, bn_gamma, bn_beta, move1_bias, prelu_a, move2_bias):
        import jax, jax.numpy as jnp
        import numpy as np
        from jax import lax
        N, C, H, W = (32, 64, 56, 56)
        K = 3
        BN_EPS = 1e-05

        def _binary_activation(x):
            sq = x * x
            o1 = jnp.where(x < -1.0, -1.0, sq + 2.0 * x)
            o2 = jnp.where(x < 0.0, o1, -sq + 2.0 * x)
            o3 = jnp.where(x < 1.0, o2, 1.0)
            return lax.stop_gradient(jnp.sign(x) - o3) + o3

        def _binarize_weights(w):
            scale = lax.stop_gradient(jnp.mean(jnp.abs(w), axis=(1, 2, 3), keepdims=True))
            cw = jnp.clip(w, -1.0, 1.0)
            return lax.stop_gradient(scale * jnp.sign(w) - cw) + cw
        out = _binary_activation(x + move0_bias)
        bw = _binarize_weights(conv_w)
        y = lax.conv_general_dilated(out, bw, window_strides=(1, 1), padding=((1, 1), (1, 1)), dimension_numbers=('NCHW', 'OIHW', 'NCHW'))
        mean = jnp.mean(y, axis=(0, 2, 3), keepdims=True)
        var = jnp.var(y, axis=(0, 2, 3), keepdims=True)
        g = bn_gamma.reshape(1, -1, 1, 1)
        b = bn_beta.reshape(1, -1, 1, 1)
        y = (y - mean) * (g / jnp.sqrt(var + BN_EPS)) + b
        y = y + x
        y = y + move1_bias
        a = prelu_a.reshape(1, -1, 1, 1)
        y = jnp.where(y >= 0.0, y, a * y)
        return y + move2_bias

    def _gn(v, G=32, eps=1e-05):
        B_, C_, H_, W_ = v.shape
        g = v.reshape(B_, G, C_ // G, H_, W_)
        m = jnp.mean(g, axis=(2, 3, 4), keepdims=True)
        s = jnp.var(g, axis=(2, 3, 4), keepdims=True)
        return ((g - m) / jnp.sqrt(s + eps)).reshape(v.shape)

    def _ln_c(v, eps=1e-06):
        m = jnp.mean(v, axis=1, keepdims=True)
        s = jnp.var(v, axis=1, keepdims=True)
        return (v - m) / jnp.sqrt(s + eps)

    def _ln_t(v, eps=1e-05):
        m = jnp.mean(v, axis=-1, keepdims=True)
        s = jnp.var(v, axis=-1, keepdims=True)
        return (v - m) / jnp.sqrt(s + eps)

    def _to_tokens(v):
        B_, C_, H_, W_ = v.shape
        return v.reshape(B_, C_, H_ * W_).transpose(0, 2, 1)

    def _from_tokens(t, like):
        B_, C_, H_, W_ = like.shape
        return t.transpose(0, 2, 1).reshape(B_, C_, H_, W_)
    x = _L0_conv_ref(x, L0_conv_W_value, L0_conv_b_value, L0_conv_W_off, L0_conv_b_off, L0_conv_W_attn, L0_conv_b_attn, L0_conv_W_out, L0_conv_b_out)
    x = _L1_conv_ref(x, L1_conv_move0_bias, L1_conv_conv_w, L1_conv_bn_gamma, L1_conv_bn_beta, L1_conv_move1_bias, L1_conv_prelu_a, L1_conv_move2_bias)
    return x

_drawn_inputs = setup_inputs


def setup_inputs(seed=0):
    import zlib

    import numpy as np

    out = dict(_drawn_inputs(seed))
    spreads = {'L0_conv_b_value': (0.0, 0.1),
     'L0_conv_b_off': (0.0, 0.1),
     'L0_conv_b_attn': (0.0, 0.51),
     'L0_conv_b_out': (0.0, 0.1),
     'L1_conv_move0_bias': (0.0, 0.1),
     'L1_conv_bn_gamma': (1.0, 0.2),
     'L1_conv_bn_beta': (0.0, 0.1),
     'L1_conv_move1_bias': (0.0, 0.1),
     'L1_conv_prelu_a': (0.25, 0.2),
     'L1_conv_move2_bias': (0.0, 0.1)}
    factors = {'L0_conv_W_attn': 4.667, 'L1_conv_conv_w': 8.0}
    for name, (base, spread) in spreads.items():
        noise = np.random.default_rng([zlib.crc32(name.encode()), seed]).standard_normal(out[name].shape)
        drawn = base * np.exp(spread * noise) if base else spread * noise
        out[name] = jnp.asarray(drawn.astype(out[name].dtype))
    for name, factor in factors.items():
        out[name] = (out[name] * factor).astype(out[name].dtype)
    return out
```

```python
from contextlib import ExitStack

import numpy as np

import concourse.bass as bass
from concourse import mybir

F32 = mybir.dt.float32
BF16 = mybir.dt.bfloat16
I32 = mybir.dt.int32
ALU = mybir.AluOpType
ACT = mybir.ActivationFunctionType
AX = mybir.AxisListType

B, C, H, W = 4, 64, 32, 32
HEADS, POINTS = 8, 4
HD = C // HEADS
HP = HEADS * POINTS
NQ = H * W
PAIR = 2
G = B // PAIR
P = PAIR * C
YH = 2
RH = H // YH
HALF = RH * W
NCH = HALF // P
TAPS = 4
NT = TAPS * TAPS
TAP0 = -2
VP = W + TAPS
CP = W + 2
K = 3
BN_EPS = 1e-5
NPRM = 8


def constants():
    j = np.arange(W)
    second = (j >= W // 2).astype(np.float64)
    pos = np.linspace(0.0, 1.0, W) * W - 0.5 - j - second
    sel = np.zeros((P, P), np.float32)
    for g in range(G):
        for i in range(PAIR):
            for h in range(HEADS):
                row = g * C + i * HP + h * POINTS
                sel[row:row + POINTS, i * C + h * HD:i * C + (h + 1) * HD] = 1.0
    eye = np.eye(C)
    avg = np.block([[eye, eye], [eye, eye]]) * 0.5
    diff = np.block([[eye, -eye], [-eye, eye]]) * 0.5
    rows = [pos, j + second, -j, [-(TAP0 + k) for k in range(TAPS)], [0.5, -1.5]]
    rows = np.tile(np.concatenate(rows)[None], (P, 1))
    return np.concatenate([rows, sel, np.eye(P), avg, diff], 1).astype(np.float32)


c_pos, c_abs, c_neg = 0, W, 2 * W
c_tap = 3 * W
c_mid = c_tap + TAPS
c_sel = c_mid + 2
c_eye = c_sel + P
c_avg = c_eye + P
c_dif = c_avg + P
NCONST = c_dif + P


def deformable_attention_then_binary_conv(nc, x, const, w_proj, w_value, w_out, b_attn, b_off, params, w_conv, w_abs, out):
    ctx = ExitStack()
    with ctx:
        def sb(name, shape, dt=F32):
            return ctx.enter_context(nc.sbuf_tensor(name, shape, dt))

        def sem(name):
            return ctx.enter_context(nc.semaphore(name))

        xs = sb("xs", [P, G, NQ])
        cst = sb("cst", [P, NCONST])
        wp = sb("wp", [P, 3, PAIR * HP])
        wv = sb("wv", [P, P])
        wo = sb("wo", [P, P])
        battn = sb("battn", [1, HP])
        ones = sb("ones", [P, P])
        boff = sb("boff", [P, 2])
        prm = sb("prm", [P, NPRM])
        wcf = sb("wcf", [P, K * K * C])
        wab = sb("wab", [P, K * K * C])
        wcb = sb("wcb", [P, K * K, P], BF16)
        vpad = sb("vpad", [P, G, VP, VP])
        u = sb("u", [P, 2, YH, HALF])
        tab = sb("tab", [P, 2, HALF])
        hat = sb("hat", [P, 2, 2 * TAPS, HALF])
        ay = sb("ay", [P, 2, TAPS, HALF])
        lsub = sb("lsub", [P, YH, HALF])
        ex = sb("ex", [P, YH, HALF])
        prob = sb("prob", [P, YH, HALF])
        lmax = sb("lmax", [P, YH, HALF // POINTS])
        lsum = sb("lsum", [P, YH, HALF // POINTS])
        lrec = sb("lrec", [P, YH, HALF // POINTS])
        AR = 4
        a = sb("a", [P, AR, HALF])
        PR = 8
        prod = sb("prod", [P, PR, G, HALF])
        sum2 = sb("sum2", [P, 2, 2, G, HALF])
        sum4 = sb("sum4", [P, 2, G, HALF])
        over = sb("over", [P, 2 * YH])
        overt = sb("overt", [P, 2, HALF])
        overs = sb("overs", [P, 2, HALF])
        flag = sb("flag", [1, 2])
        flagi = sb("flagi", [1, 1], I32)
        x1 = sb("x1", [P, G, NQ])
        sg = sb("sg", [P, G, CP, CP], BF16)
        wabs = sb("wabs", [P, K * K * C])
        bns = sb("bns", [P, G * YH, 6])
        mv = sb("mv", [P, 2])
        st = sb("st", [P, 16])
        spare = prod[:].rearrange("p r g n -> p (r g n)")

        def share(i, n, of=spare):
            return of[:, i * NQ:(i + n) * NQ]

        zz, zr, zq, res = (share(2 * i, 2).rearrange("p (g n) -> p g n", g=G) for i in range(4))
        gxy = share(0, 2).rearrange("p (d n) -> p d n", d=2)
        gt = share(2, 2).rearrange("p (d n) -> p d n", d=2)
        gatt, gay, ga = share(4, 1), share(5, 1), share(6, 1)
        gacc = share(0, 2, sum2[:].rearrange("p m j g n -> p (m j g n)")).rearrange("p (g n) -> p g n", g=G)

        bank = [ctx.enter_context(nc.psum_tensor(f"bank{i}", [P, HALF], F32)) for i in range(8)]
        ps_out = [[bank[0], bank[1]], [bank[2], bank[3]]]
        ps_w = [[bank[6], bank[7]], [bank[4], bank[5]]]
        ps_y = [[bank[4], bank[5]], [bank[6], bank[7]]]
        ps_v = [[bank[0], bank[1]], [bank[2], bank[3]]]
        ps_off = [[bank[4], bank[5]], [bank[2], bank[3]]]
        ps_log = [bank[6], bank[2]]
        ps_att = [bank[4], bank[3]]

        s_x = [sem(f"x_in{g}") for g in range(G)]
        s_cst = sem("const_in")
        s_wp = sem("proj_in")
        s_wv = sem("value_w_in")
        s_prm = sem("params_in")
        s_late = sem("late_weights_in")
        s_zero = sem("memsets_done")
        s_off = sem("offsets_ready")
        s_log = sem("logits_ready")
        s_v = sem("values_ready")
        s_vp = sem("values_stored")
        s_u = sem("positions_ready")
        s_abs = sem("abs_ready")
        s_hat = sem("hats_ready")
        s_exp = sem("exp_ready")
        s_max = sem("max_ready")
        s_sub = sem("sub_ready")
        s_sum = sem("sums_ready")
        s_rec = sem("recips_ready")
        s_prob = sem("probs_ready")
        s_att = sem("probs_turned")
        s_ay = sem("ay_ready")
        s_a = sem("tap_weights_ready")
        s_w = sem("spread_ready")
        s_p = sem("products_ready")
        s_s2 = sem("pair_sums_ready")
        s_s4 = sem("row_sums_ready")
        s_o = sem("projected")
        s_ov1 = sem("over_abs")
        s_ov = sem("over_ready")
        s_fps = sem("flag_summed")
        s_f1 = sem("flag_steps")
        s_flag = sem("flag_ready")
        s_x1 = sem("x1_ready")
        s_sg = sem("signs_ready")
        s_wc = sem("conv_weights_ready")
        s_wab = sem("abs_weights_ready")
        s_pre = sem("bn_constants")
        s_y = sem("conv_ready")
        s_bns = sem("bn_stats_done")
        s_mv = sem("bn_aggregated")
        s_pair = sem("bn_paired")
        s_st = sem("bn_steps")
        s_sd = sem("bn_root")
        s_k = sem("bn_scale_ready")
        s_z = sem("z_ready")
        s_r = sem("relu_ready")
        s_q = sem("line_ready")
        s_res = sem("result_ready")
        s_done = sem("stored")
        s_ga = sem("g_weights_ready")
        s_gw = sem("g_spread_ready")
        s_gt = sem("g_probs_turned")
        s_gd = sem("g_steps")
        s_gc = sem("g_accumulated")
        s_go = sem("g_projected")
        s_gx = sem("g_x1_ready")
        s_gs = sem("g_signs_ready")

        def chunk(t, g, yh):
            return t[:, g, yh * HALF:(yh + 1) * HALF]

        def rows(ap):
            return ap.rearrange("p (y x) -> p y x", x=W)

        def along(ap, d):
            n = ap.shape[1]
            return ap.unsqueeze(1).to_broadcast([P, RH, n]) if d == 0 else ap.unsqueeze(2).to_broadcast([P, n, W])

        def sel_of(g):
            return cst[g * C:(g + 1) * C, c_sel:c_sel + P]

        def v_window(g, yh, ky, kx):
            y0 = yh * RH + ky + yh
            r = vpad[:, g, y0:y0 + RH, kx:kx + W + 1]
            return bass.AP(r.tensor, r.offset, [r.ap[0], [VP, RH], [W // 2 + 1, 2], [1, W // 2]])

        def by_col_half(ap):
            return ap.rearrange("p (y a x) -> p y a x", a=2, x=W // 2)

        block = ctx.enter_context(nc.Block())

        @block.sync
        def _(sp):
            for g in range(G):
                sp.dma_start(xs[:, g, :], x[PAIR * g:PAIR * (g + 1)].rearrange("b c h w -> (b c) (h w)")).then_inc(s_x[g], 16)
            sp.dma_start(wv[:], w_value).then_inc(s_wv, 16)
            sp.dma_start(prm[:], params).then_inc(s_prm, 16)
            sp.dma_start(wo[:], w_out).then_inc(s_late, 16)
            sp.dma_start(wcf[:], w_conv).then_inc(s_late, 16)
            sp.dma_start(wab[:], w_abs).then_inc(s_late, 16)
            n = 0
            for yh in range(YH):
                for g in range(G):
                    n += 1
                    sp.wait_ge(s_res, n)
                    dst = out[PAIR * g:PAIR * (g + 1)].rearrange("b c h w -> (b c) (h w)")
                    sp.dma_start(dst[:, yh * HALF:(yh + 1) * HALF], chunk(res, g, yh)).then_inc(s_done, 16)
            sp.wait_ge(s_done, 16 * G * YH)

        @block.tensor
        def _(pe):
            def offsets(yh):
                for d in range(2):
                    for g in range(G):
                        mm = pe.matmul(ps_off[yh][d][g * C:(g + 1) * C, :], wp[:, d, :], chunk(xs, g, yh), start=True, stop=True)
                    mm.then_inc(s_off, 1)

            def logits(yh):
                pe.matmul(ps_log[yh][:], ones[0:1, :], battn[0:1, :].unsqueeze(1).to_broadcast([1, HALF // HP, HP]),
                          start=True, stop=False, skip_group_check=True)
                for n in range(NCH):
                    for g in range(G):
                        at = n * P + g * C
                        q = yh * HALF + n * P
                        mm = pe.matmul(ps_log[yh][:, at:at + C], xs[:, g, q:q + P], wp[:, 2, :], start=False,
                                       stop=(n == NCH - 1 and g == G - 1), skip_group_check=True)
                mm.then_inc(s_log, 1)

            def turn(yh):
                pe.wait_ge(s_prob, yh + 1)
                for n in range(NCH):
                    mm = pe.transpose(ps_att[yh][:, n * P:(n + 1) * P], prob[:, yh, n * P:(n + 1) * P], cst[:, c_eye:c_eye + P])
                mm.then_inc(s_att, 1)

            def spread(t):
                pe.wait_ge(s_a, t + 1)
                for g in range(G):
                    if t >= 2:
                        pe.wait_ge(s_p, 2 * (t - 2) + g + 1)
                    pe.matmul(ps_w[t % 2][g][:], sel_of(g), a[g * C:(g + 1) * C, t % AR, :], start=True, stop=True).then_inc(s_w, 1)

            def project(m):
                yh, ky = divmod(m, TAPS)
                pe.wait_ge(s_s4, m + 1)
                if yh == 0 and ky == 0:
                    pe.wait_ge(s_late, 48)
                for g in range(G):
                    mm = pe.matmul(ps_out[yh][g][:], wo[:], sum4[:, m % 2, g, :], start=(ky == 0), stop=(ky == TAPS - 1))
                mm.then_inc(s_o, 1)

            pe.wait_ge(s_wp, 16)
            pe.wait_ge(s_x[0], 16)
            pe.wait_ge(s_x[1], 16)
            offsets(0)
            pe.wait_ge(s_zero, 1)
            pe.wait_ge(s_prm, 48)
            logits(0)
            pe.wait_ge(s_wv, 16)
            for yh in range(YH):
                for g in range(G):
                    pe.matmul(ps_v[yh][g][:], wv[:], chunk(xs, g, yh), start=True, stop=True).then_inc(s_v, 1)
            pe.wait_ge(s_vp, 4)
            offsets(1)
            pe.wait_ge(s_cst, 16)
            pe.wait_ge(s_u, 1)
            turn(0)
            for t in range(NT * YH):
                if t == 1:
                    pe.wait_ge(s_ay, TAPS)
                spread(t)
                if t == 2:
                    pe.wait_ge(s_u, 4)
                    logits(1)
                if t == 9:
                    turn(1)
                if t == 11:
                    pe.wait_ge(s_ov, 4)
                    pe.wait_ge(s_sub, 2)
                    pe.matmul(ps_log[1][0:1, 0:4], ones[:, 0:1], over[:], start=True, stop=True).then_inc(s_fps, 1)
                if t % TAPS == TAPS - 2 and t > TAPS:
                    if t // TAPS - 1 == TAPS:
                        pe.wait_ge(s_ay, 2 * TAPS)
                    project(t // TAPS - 1)
            project(TAPS * YH - 1)

            pe.wait_ge(s_flag, 1)
            beyond = pe.value_load(flagi[0:1, 0:1], min_val=0, max_val=1)
            with pe.If(beyond > 0):
                pe.wait_ge(s_x1, 4)
                for n in range(2 * NCH):
                    mm = pe.transpose(bank[n // NCH][:, (n % NCH) * P:(n % NCH + 1) * P],
                                      prob[:, n // NCH, (n % NCH) * P:(n % NCH + 1) * P], cst[:, c_eye:c_eye + P])
                mm.then_inc(s_gt, 1)
                with pe.Fori(0, NQ) as key:
                    pe.wait_ge(s_ga, key + 1)
                    for g in range(G):
                        for yh in range(YH):
                            mm = pe.matmul(bank[4 + 2 * yh + g][:], sel_of(g), ga[g * C:(g + 1) * C, yh * HALF:(yh + 1) * HALF],
                                           start=True, stop=True)
                    mm.then_inc(s_gw, 1)
                pe.wait_ge(s_gc, 1)
                for yh in range(YH):
                    for g in range(G):
                        mm = pe.matmul(ps_out[yh][g][:], wo[:], chunk(gacc, g, yh), start=True, stop=True)
                mm.then_inc(s_go, 1)
                pe.wait_ge(s_gs, 4)
            pe.end_ifs()

            pe.wait_ge(s_wc, 2)
            pe.wait_ge(s_sg, 4)
            pe.wait_ge(s_p, 2 * NT * YH)
            for yh in range(YH):
                for g in range(G):
                    for k in range(K * K):
                        y0, x0 = yh * RH + k // K, k % K
                        mm = pe.matmul(ps_y[yh][g][:], wcb[:, k, :], sg[:, g, y0:y0 + RH, x0:x0 + W],
                                       start=(k == 0), stop=(k == K * K - 1))
                    mm.then_inc(s_y, 1)
            pe.wait_ge(s_mv, 1)
            pe.matmul(bank[0][:, 0:2], cst[:, c_avg:c_avg + P], mv[:, 0:2], start=True, stop=True)
            pe.matmul(bank[0][:, 2:3], cst[:, c_dif:c_dif + P], mv[:, 0:1], start=True, stop=True,
                      skip_group_check=True).then_inc(s_pair, 1)

        @block.scalar
        def _(act):
            act.dma_start(wp[:], w_proj).then_inc(s_wp, 16)
            act.dma_start(cst[:], const).then_inc(s_cst, 16)
            act.dma_start(boff[:], b_off).then_inc(s_prm, 16)
            act.dma_start(battn[:], b_attn).then_inc(s_prm, 16)

            done = 0

            def hats(yh, d, taps):
                nonlocal done
                for k in taps:
                    place = done % 2
                    if done >= 2:
                        act.wait_ge(s_hat, done - 1)
                    nc.scalar.activation(tab[:, place, :], u[:, d, yh, :], ACT.Abs,
                                         bias=cst[:, c_tap + k:c_tap + k + 1]).then_inc(s_abs, 1)
                    done += 1
                    act.wait_ge(s_abs, done)
                    nc.scalar.activation(hat[:, yh, d * TAPS + k, :], tab[:, place, :], ACT.Relu, bias=1.0, scale=-1.0).then_inc(s_hat, 1)

            act.wait_ge(s_cst, 16)
            act.wait_ge(s_u, 1)
            hats(0, 0, [0])
            act.wait_ge(s_u, 2)
            hats(0, 1, [0])
            act.wait_ge(s_sub, 1)
            nc.scalar.activation(ex[:, 0, :], lsub[:, 0, :], ACT.Exp).then_inc(s_exp, 1)
            act.wait_ge(s_prm, 48)
            act.wait_ge(s_zero, 2)
            for n in range(G * YH):
                yh, g = divmod(n, G)
                act.wait_ge(s_v, n + 1)
                y0 = yh * RH - TAP0
                nc.scalar.activation(vpad[:, g, y0:y0 + RH, -TAP0:W - TAP0], rows(ps_v[yh][g][:]), ACT.Identity,
                                     bias=prm[:, 0:1]).then_inc(s_vp, 1)
            hats(0, 0, [1, 2, 3])
            hats(0, 1, [1, 2, 3])
            act.wait_ge(s_u, 4)
            hats(1, 0, range(TAPS))
            hats(1, 1, range(TAPS))
            act.wait_ge(s_sub, 2)
            nc.scalar.activation(ex[:, 1, :], lsub[:, 1, :], ACT.Exp).then_inc(s_exp, 1)
            for n in range(2 * YH):
                yh, d = divmod(n, 2)
                if n >= 2:
                    act.wait_ge(s_ov, n - 1)
                nc.scalar.activation(overt[:, n % 2, :], u[:, d, yh, :], ACT.Abs, bias=cst[:, c_mid:c_mid + 1]).then_inc(s_ov1, 1)
                act.wait_ge(s_ov1, n + 1)
                nc.scalar.activation(overs[:, n % 2, :], overt[:, n % 2, :], ACT.Relu, bias=cst[:, c_mid + 1:c_mid + 2],
                                     accum_out=over[:, n:n + 1]).then_inc(s_ov, 1)
            act.wait_ge(s_late, 48)
            act.wait_ge(s_zero, 3)
            for i in range(PAIR):
                at = slice(i * C, (i + 1) * C)
                nc.scalar.activation(wcb[at, :, at], wcf[at, :].rearrange("p (k c) -> p k c", k=K * K), ACT.Sign).then_inc(s_wc, 1)
            nc.scalar.activation(wabs[:], wab[:], ACT.Abs, accum_out=st[:, 0:1]).then_inc(s_wab, 1)
            act.wait_ge(s_zero, 4)
            act.wait_ge(s_wab, 1)

            def signs(wait_on, done):
                for n in range(G * YH):
                    yh, g = divmod(n, G)
                    act.wait_ge(wait_on, n + 1)
                    nc.scalar.activation(sg[:, g, 1 + yh * RH:1 + (yh + 1) * RH, 1:1 + W], rows(chunk(x1, g, yh)), ACT.Sign,
                                         bias=prm[:, 2:3]).then_inc(done, 1)

            signs(s_x1, s_sg)
            act.wait_ge(s_flag, 1)
            beyond = act.value_load(flagi[0:1, 0:1], min_val=0, max_val=1)
            with act.If(beyond > 0):
                signs(s_gx, s_gs)
            act.end_ifs()
            nc.scalar.activation(st[:, 14:15], ones[:, 0:1], ACT.Sqrt)
            act.wait_ge(s_st, 3)
            nc.scalar.activation(st[:, 8:9], st[:, 7:8], ACT.Sqrt).then_inc(s_sd, 1)
            act.wait_ge(s_k, 3)
            for n in range(G * YH):
                yh, g = divmod(n, G)
                act.wait_ge(s_z, n + 1)
                nc.scalar.activation(chunk(zr, g, yh), chunk(zz, g, yh), ACT.Relu, bias=st[:, 12:13]).then_inc(s_r, 1)
                nc.scalar.activation(chunk(zq, g, yh), chunk(zz, g, yh), ACT.Identity, bias=st[:, 13:14],
                                     scale=prm[:, 6:7]).then_inc(s_q, 1)

        @block.gpsimd
        def _(pool):
            pool.memset(ones[:], 1.0).then_inc(s_zero, 1)
            pool.memset(vpad[:].rearrange("p g y x -> p (g y x)"), 0.0).then_inc(s_zero, 1)
            pool.memset(wcb[:].rearrange("p k c -> p (k c)"), 0.0).then_inc(s_zero, 1)
            pool.memset(sg[:].rearrange("p g y x -> p (g y x)"), 0.0).then_inc(s_zero, 1)
            for m in range(TAPS * YH):
                for j in range(2):
                    t = TAPS * m + 2 * j
                    pool.wait_ge(s_p, 2 * (t + 2))
                    if m >= 2:
                        pool.wait_ge(s_s4, m - 1)
                    pool.tensor_tensor(sum2[:, m % 2, j], prod[:, t % PR], prod[:, (t + 1) % PR], ALU.add).then_inc(s_s2, 1)
                pool.wait_ge(s_s2, 2 * m + 2)
                if m >= 2:
                    pool.wait_ge(s_o, m - 1)
                pool.tensor_tensor(sum4[:, m % 2], sum2[:, m % 2, 0], sum2[:, m % 2, 1], ALU.add).then_inc(s_s4, 1)

        @block.vector
        def _(dve):
            def positions(yh):
                for d in range(2):
                    n = 2 * yh + d
                    dve.wait_ge(s_off, n + 1)
                    at = cst[:, c_pos:c_pos + W] if d == 0 else cst[:, c_pos + yh * RH:c_pos + (yh + 1) * RH]
                    nc.vector.scalar_tensor_tensor(out=rows(u[:, d, yh, :]), in0=rows(ps_off[yh][d][:]), scalar=boff[:, d:d + 1],
                                                   in1=along(at, d), op0=ALU.add, op1=ALU.add).then_inc(s_u, 1)

            def grouped(ap):
                return ap.rearrange("p (n k) -> p n k", k=POINTS)

            def spread_points(ap):
                return ap.unsqueeze(2).to_broadcast([P, HALF // POINTS, POINTS])

            def softmax_head(yh):
                dve.wait_ge(s_log, yh + 1)
                nc.vector.tensor_reduce(lmax[:, yh, :], grouped(ps_log[yh][:]), AX.X, ALU.max).then_inc(s_max, 1)
                dve.wait_ge(s_max, yh + 1)
                nc.vector.tensor_tensor(grouped(lsub[:, yh, :]), grouped(ps_log[yh][:]), spread_points(lmax[:, yh, :]),
                                        ALU.subtract).then_inc(s_sub, 1)

            def softmax_tail(yh):
                dve.wait_ge(s_exp, yh + 1)
                nc.vector.tensor_reduce(lsum[:, yh, :], grouped(ex[:, yh, :]), AX.X, ALU.add).then_inc(s_sum, 1)
                dve.wait_ge(s_sum, yh + 1)
                nc.vector.reciprocal(lrec[:, yh, :], lsum[:, yh, :]).then_inc(s_rec, 1)
                dve.wait_ge(s_rec, yh + 1)
                nc.vector.tensor_tensor(grouped(prob[:, yh, :]), grouped(ex[:, yh, :]), spread_points(lrec[:, yh, :]),
                                        ALU.mult).then_inc(s_prob, 1)

            def attend(yh, ky):
                dve.wait_ge(s_att, yh + 1)
                dve.wait_ge(s_hat, (2 if ky == 0 else 5 + ky) if yh == 0 else 13 + ky)
                nc.vector.tensor_tensor(ay[:, yh, ky, :], ps_att[yh][:], hat[:, yh, TAPS + ky, :], ALU.mult).then_inc(s_ay, 1)

            def weight(t):
                yh, k = divmod(t, NT)
                ky, kx = divmod(k, TAPS)
                dve.wait_ge(s_ay, yh * TAPS + ky + 1)
                dve.wait_ge(s_hat, (1 if kx == 0 else 2 + kx) if yh == 0 else 9 + kx)
                if t >= AR:
                    dve.wait_ge(s_w, 2 * (t - AR + 1))
                nc.vector.tensor_tensor(a[:, t % AR, :], ay[:, yh, ky, :], hat[:, yh, kx, :], ALU.mult).then_inc(s_a, 1)

            def product(t):
                yh, k = divmod(t, NT)
                ky, kx = divmod(k, TAPS)
                if t == 0:
                    dve.wait_ge(s_vp, 4)
                if t >= PR:
                    dve.wait_ge(s_s2, (t - PR) // 2 + 1)
                for g in range(G):
                    dve.wait_ge(s_w, 2 * t + g + 1)
                    nc.vector.tensor_tensor(by_col_half(prod[:, t % PR, g, :]), by_col_half(ps_w[t % 2][g][:]),
                                            v_window(g, yh, ky, kx), ALU.mult).then_inc(s_p, 1)

            def residual(yh, done):
                for g in range(G):
                    nc.vector.scalar_tensor_tensor(out=chunk(x1, g, yh), in0=ps_out[yh][g][:], scalar=prm[:, 1:2],
                                                   in1=chunk(xs, g, yh), op0=ALU.add, op1=ALU.add).then_inc(done, 1)

            dve.wait_ge(s_cst, 16)
            dve.wait_ge(s_prm, 48)
            positions(0)
            softmax_head(0)
            softmax_tail(0)
            positions(1)
            attend(0, 0)
            weight(0)
            weight(1)
            for ky in range(1, TAPS):
                attend(0, ky)
            for t in range(NT * YH):
                if t == 5:
                    softmax_head(1)
                if t == 8:
                    softmax_tail(1)
                if 11 <= t < 11 + TAPS:
                    attend(1, t - 11)
                if t == 13:
                    dve.wait_ge(s_fps, 1)
                    nc.vector.reduce_sum(flag[:, 0:1], ps_log[1][0:1, 0:4], AX.X).then_inc(s_f1, 1)
                if t == 15:
                    dve.wait_ge(s_f1, 1)
                    nc.vector.tensor_scalar(flagi[:], flag[:, 0:1], 0.0, None, ALU.is_gt).then_inc(s_flag, 1)
                if t == 16:
                    dve.wait_ge(s_wab, 1)
                    nc.vector.tensor_scalar(st[:, 1:2], st[:, 0:1], 1.0 / (K * K * C), None, ALU.mult).then_inc(s_pre, 1)
                    nc.vector.tensor_tensor(st[:, 4:5], prm[:, 4:5], prm[:, 5:6], ALU.add).then_inc(s_pre, 1)
                    nc.vector.tensor_scalar(st[:, 5:6], prm[:, 6:7], -1.0, 1.0, ALU.mult, ALU.add).then_inc(s_pre, 1)
                    dve.wait_ge(s_pre, 3)
                    nc.vector.tensor_tensor(st[:, 2:3], st[:, 1:2], st[:, 1:2], ALU.mult).then_inc(s_pre, 1)
                    nc.vector.tensor_tensor(st[:, 3:4], st[:, 1:2], prm[:, 3:4], ALU.mult).then_inc(s_pre, 1)
                if t + 2 < NT * YH:
                    weight(t + 2)
                product(t)
                if t == NT + 6:
                    dve.wait_ge(s_o, TAPS)
                    residual(0, s_x1)
            dve.wait_ge(s_o, TAPS * YH)
            residual(1, s_x1)

            beyond = dve.value_load(flagi[0:1, 0:1], min_val=0, max_val=1)
            with dve.If(beyond > 0):
                dve.wait_ge(s_gt, 1)
                for yh in range(YH):
                    nc.vector.tensor_copy(gatt[:, yh * HALF:(yh + 1) * HALF], bank[yh][:]).then_inc(s_gd, 1)
                    for d in range(2):
                        at = cst[:, c_abs:c_abs + W] if d == 0 else cst[:, c_abs + yh * RH:c_abs + (yh + 1) * RH]
                        nc.vector.tensor_tensor(rows(gxy[:, d, yh * HALF:(yh + 1) * HALF]), rows(u[:, d, yh, :]), along(at, d),
                                                ALU.add).then_inc(s_gd, 1)
                nc.vector.memset(gacc[:].rearrange("p g n -> p (g n)"), 0.0).then_inc(s_gd, 1)

                def general_hat(axis, key, times, into, base, done):
                    dve.wait_ge(s_gd, base)
                    nc.vector.tensor_scalar(gt[:, 0, :], gxy[:, axis, :], cst[:, bass.ds(c_neg + key, 1)], 1.0, ALU.add,
                                            ALU.add).then_inc(s_gd, 1)
                    dve.wait_ge(s_gd, base + 1)
                    nc.vector.tensor_scalar(gt[:, 1, :], gt[:, 0, :], -1.0, 2.0, ALU.mult, ALU.add).then_inc(s_gd, 1)
                    dve.wait_ge(s_gd, base + 2)
                    nc.vector.tensor_tensor(gt[:, 0, :], gt[:, 0, :], gt[:, 1, :], ALU.min).then_inc(s_gd, 1)
                    dve.wait_ge(s_gd, base + 3)
                    nc.vector.scalar_tensor_tensor(out=into, in0=gt[:, 0, :], scalar=0.0, in1=times, op0=ALU.max,
                                                   op1=ALU.mult).then_inc(done, 1)

                SETUP, PER_Y, PER_X = 7, 4, 3 + G * YH
                with dve.Fori(0, H) as key_y:
                    at_y = SETUP + key_y * (PER_Y + PER_X * W)
                    general_hat(1, key_y, gatt, gay, at_y, s_gd)
                    with dve.Fori(0, W) as key_x:
                        at_x = at_y + PER_Y + PER_X * key_x
                        general_hat(0, key_x, gay, ga, at_x, s_ga)
                        dve.wait_ge(s_gw, W * key_y + key_x + 1)
                        for g in range(G):
                            value = vpad[:, g].rearrange("p y x -> p (y x)")[
                                :, bass.ds(key_y * VP + key_x + (VP + 1) * -TAP0, 1)]
                            for yh in range(YH):
                                nc.vector.scalar_tensor_tensor(out=chunk(gacc, g, yh), in0=bank[4 + 2 * yh + g][:], scalar=value,
                                                               in1=chunk(gacc, g, yh), op0=ALU.mult, op1=ALU.add).then_inc(s_gd, 1)
                dve.wait_ge(s_gd, SETUP + H * (PER_Y + PER_X * W))
                dve.sem_inc(s_gc, 1)
                dve.wait_ge(s_go, 1)
                dve.wait_ge(s_sg, 4)
                for yh in range(YH):
                    residual(yh, s_gx)
            dve.end_ifs()

            for n in range(G * YH):
                yh, g = divmod(n, G)
                dve.wait_ge(s_y, n + 1)
                nc.vector.bn_stats(bns[:, n, :], ps_y[yh][g][:]).then_inc(s_bns, 1)
            dve.wait_ge(s_bns, G * YH)
            nc.vector.bn_aggr(mv[:], bns[:].rearrange("p n s -> p (n s)")).then_inc(s_mv, 1)
            dve.wait_ge(s_pair, 1)
            nc.vector.tensor_copy(st[:, 9:12], bank[0][:, 0:3]).then_inc(s_st, 1)
            dve.wait_ge(s_st, 1)
            dve.wait_ge(s_pre, 5)
            nc.vector.scalar_tensor_tensor(out=st[:, 6:7], in0=st[:, 11:12], scalar=st[:, 11:12], in1=st[:, 10:11], op0=ALU.mult,
                                           op1=ALU.add).then_inc(s_st, 1)
            dve.wait_ge(s_st, 2)
            nc.vector.tensor_scalar(st[:, 7:8], st[:, 6:7], st[:, 2:3], BN_EPS, ALU.mult, ALU.add).then_inc(s_st, 1)
            dve.wait_ge(s_sd, 1)
            nc.vector.reciprocal(st[:, 6:7], st[:, 8:9]).then_inc(s_st, 1)
            dve.wait_ge(s_st, 4)
            nc.vector.scalar_tensor_tensor(out=st[:, 8:9], in0=st[:, 6:7], scalar=st[:, 6:7], in1=st[:, 7:8], op0=ALU.mult,
                                           op1=ALU.mult).then_inc(s_st, 1)
            dve.wait_ge(s_st, 5)
            nc.vector.tensor_scalar(st[:, 11:12], st[:, 8:9], -0.5, 1.5, ALU.mult, ALU.add).then_inc(s_st, 1)
            dve.wait_ge(s_st, 6)
            nc.vector.scalar_tensor_tensor(out=st[:, 10:11], in0=st[:, 11:12], scalar=st[:, 6:7], in1=st[:, 3:4], op0=ALU.mult,
                                           op1=ALU.mult).then_inc(s_k, 1)
            dve.wait_ge(s_k, 1)
            nc.vector.scalar_tensor_tensor(out=st[:, 12:13], in0=st[:, 9:10], scalar=st[:, 10:11], in1=st[:, 4:5], op0=ALU.mult,
                                           op1=ALU.subtract, reverse1=True).then_inc(s_k, 1)
            dve.wait_ge(s_k, 2)
            nc.vector.tensor_scalar(st[:, 13:14], st[:, 12:13], prm[:, 6:7], prm[:, 7:8], ALU.mult, ALU.add).then_inc(s_k, 1)

            def scaled(n):
                yh, g = divmod(n, G)
                nc.vector.scalar_tensor_tensor(out=chunk(zz, g, yh), in0=ps_y[yh][g][:], scalar=st[:, 10:11], in1=chunk(x1, g, yh),
                                               op0=ALU.mult, op1=ALU.add).then_inc(s_z, 1)

            def prelu(n):
                yh, g = divmod(n, G)
                dve.wait_ge(s_r, n + 1)
                dve.wait_ge(s_q, n + 1)
                nc.vector.scalar_tensor_tensor(out=chunk(res, g, yh), in0=chunk(zr, g, yh), scalar=st[:, 5:6], in1=chunk(zq, g, yh),
                                               op0=ALU.mult, op1=ALU.add).then_inc(s_res, 1)

            for n in range(G * YH):
                scaled(n)
                if n >= 2:
                    prelu(n - 2)
            prelu(2)
            prelu(3)


def kernel(**inputs):
    import concourse.bacc as _bacc
    from concourse.bass_utils import run_bass_kernel_spmd as _run

    def get(name):
        return np.ascontiguousarray(inputs[name])

    def blocks(w):
        out = np.zeros((P, w.shape[1] * PAIR), w.dtype)
        for i in range(PAIR):
            out[i * w.shape[0]:(i + 1) * w.shape[0], i * w.shape[1]:(i + 1) * w.shape[1]] = w
        return out

    w_off = get("L0_conv_W_off").reshape(C, HP, 2)
    w_proj = np.stack([blocks(w_off[:, :, 0]), blocks(w_off[:, :, 1]), blocks(get("L0_conv_W_attn"))], 1)
    conv_w = get("L1_conv_conv_w")
    params = [get(n).reshape(C) for n in ("L0_conv_b_value", "L0_conv_b_out", "L1_conv_move0_bias", "L1_conv_bn_gamma",
                                          "L1_conv_bn_beta", "L1_conv_move1_bias", "L1_conv_prelu_a", "L1_conv_move2_bias")]
    arrays = {
        "x": get("x"),
        "const": constants(),
        "w_proj": w_proj,
        "w_value": blocks(get("L0_conv_W_value")),
        "w_out": blocks(get("L0_conv_W_out")),
        "b_attn": get("L0_conv_b_attn").reshape(1, HP),
        "b_off": np.tile(get("L0_conv_b_off").reshape(HP, 2), (B, 1)),
        "params": np.tile(np.stack(params, 1), (PAIR, 1)),
        "w_conv": np.tile(conv_w.transpose(1, 2, 3, 0).reshape(C, K * K * C), (PAIR, 1)),
        "w_abs": np.tile(conv_w.reshape(C, C * K * K), (PAIR, 1)),
    }
    arrays = {n + "_dram": np.ascontiguousarray(v) for n, v in arrays.items()}
    nc = _bacc.Bacc("TRN2", target_bir_lowering=False, num_devices=1)
    args = [nc.dram_tensor(n, v.shape, F32, kind="ExternalInput").ap() for n, v in arrays.items()]
    args.append(nc.dram_tensor("out_dram", (B, C, H, W), F32, kind="ExternalOutput").ap())
    deformable_attention_then_binary_conv(nc, *args)
    r = _run(nc, [arrays], core_ids=[0])
    return r.results[0]["out_dram"]
```

```python
from contextlib import ExitStack

import numpy as np

import concourse.bass as bass
from concourse import mybir

F32 = mybir.dt.float32
BF16 = mybir.dt.bfloat16
I32 = mybir.dt.int32
ALU = mybir.AluOpType
ACT = mybir.ActivationFunctionType
AX = mybir.AxisListType

B, C, H, W = 4, 64, 32, 32
HEADS, POINTS = 8, 4
HD = C // HEADS
HP = HEADS * POINTS
NQ = H * W
PAIR = 2
G = B // PAIR
P = PAIR * C
YH = 2
RH = H // YH
HALF = RH * W
NCH = HALF // P
TAPS = 4
NT = TAPS * TAPS
TAP0 = -2
VP = W + TAPS
CP = W + 2
K = 3
BN_EPS = 1e-5
p_bv, p_bo, p_move0, p_gamma, p_beta, p_move1, p_prelu, p_move2 = range(8)
p_off = 8
p_att = p_off + 2
NPRM = p_att + HP


def constants():
    j = np.arange(W)
    second = (j >= W // 2).astype(np.float64)
    pos = np.linspace(0.0, 1.0, W) * W - 0.5 - j - second
    sel = np.zeros((P, P), np.float32)
    for g in range(G):
        for i in range(PAIR):
            for h in range(HEADS):
                row = g * C + i * HP + h * POINTS
                sel[row:row + POINTS, i * C + h * HD:i * C + (h + 1) * HD] = 1.0
    eye = np.eye(C)
    avg = np.block([[eye, eye], [eye, eye]]) * 0.5
    diff = np.block([[eye, -eye], [-eye, eye]]) * 0.5
    rows = [pos, j + second, -j, [-(TAP0 + k) for k in range(TAPS)], [0.5, -1.5]]
    rows = np.tile(np.concatenate(rows)[None], (P, 1))
    return np.concatenate([rows, sel, np.eye(P), avg, diff], 1).astype(np.float32)


c_pos, c_abs, c_neg = 0, W, 2 * W
c_tap = 3 * W
c_mid = c_tap + TAPS
c_sel = c_mid + 2
c_eye = c_sel + P
c_avg = c_eye + P
c_dif = c_avg + P
NCONST = c_dif + P


def deformable_attention_then_binary_conv(nc, x, const, w_in, w_out, params, w_conv, w_abs, out):
    ctx = ExitStack()
    with ctx:
        def sb(name, shape, dt=F32):
            return ctx.enter_context(nc.sbuf_tensor(name, shape, dt))

        def sem(name):
            return ctx.enter_context(nc.semaphore(name))

        xs = sb("xs", [P, G, NQ])
        cst = sb("cst", [P, NCONST])
        win = sb("win", [P, 3 * PAIR * HP + P])
        wp = win[:, 0:3 * PAIR * HP].rearrange("p (k n) -> p k n", k=3)
        wv = win[:, 3 * PAIR * HP:]
        wo = sb("wo", [P, P])
        ones = sb("ones", [P, P])
        prm = sb("prm", [P, NPRM])
        wcf = sb("wcf", [P, K * K * C])
        wab = sb("wab", [P, K * K * C])
        wcb = sb("wcb", [P, K * K, P], BF16)
        vpad = sb("vpad", [P, G, VP, VP])
        u = sb("u", [P, 2, YH, HALF])
        tab = sb("tab", [P, 3, HALF])
        hat = sb("hat", [P, 2, 2 * TAPS, HALF])
        ay = sb("ay", [P, 2, TAPS, HALF])
        lsub = sb("lsub", [P, YH, HALF])
        ex = sb("ex", [P, YH, HALF])
        prob = sb("prob", [P, YH, HALF])
        lmax = sb("lmax", [P, YH, HALF // POINTS])
        lsum = sb("lsum", [P, YH, HALF // POINTS])
        lrec = sb("lrec", [P, YH, HALF // POINTS])
        AR = 4
        a = sb("a", [P, AR, HALF])
        PR = 8
        prod = sb("prod", [P, PR, G, HALF])
        sum2 = sb("sum2", [P, 2, 2, G, HALF])
        sum4 = sb("sum4", [P, 2, G, HALF])
        over = sb("over", [P, 2 * YH])
        overt = sb("overt", [P, 2, HALF])
        overs = sb("overs", [P, 2, HALF])
        flag = sb("flag", [1, 2])
        flagi = sb("flagi", [1, 1], I32)
        x1 = sb("x1", [P, G, NQ])
        sg = sb("sg", [P, G, CP, CP], BF16)
        wabs = sb("wabs", [P, K * K * C])
        bns = sb("bns", [P, G * YH, 6])
        mv = sb("mv", [P, 2])
        st = sb("st", [P, 16])
        spare = prod[:].rearrange("p r g n -> p (r g n)")

        def share(i, n, of=spare):
            return of[:, i * NQ:(i + n) * NQ]

        zz, zr, zq, res = (share(2 * i, 2).rearrange("p (g n) -> p g n", g=G) for i in range(4))
        gxy = share(0, 2).rearrange("p (d n) -> p d n", d=2)
        gt = share(2, 2).rearrange("p (d n) -> p d n", d=2)
        gatt, gay, ga = share(4, 1), share(5, 1), share(6, 1)
        gacc = share(0, 2, sum2[:].rearrange("p m j g n -> p (m j g n)")).rearrange("p (g n) -> p g n", g=G)

        bank = [ctx.enter_context(nc.psum_tensor(f"bank{i}", [P, HALF], F32)) for i in range(8)]
        ps_out = [[bank[0], bank[1]], [bank[2], bank[3]]]
        ps_w = [[bank[4], bank[5]], [bank[6], bank[7]]]
        ps_y = [[bank[4], bank[5]], [bank[6], bank[7]]]
        ps_v = [[bank[0], bank[1]], [bank[2], bank[3]]]
        ps_off = [[bank[4], bank[5]], [bank[2], bank[3]]]
        ps_log = [bank[6], bank[7]]
        ps_att = [bank[0], bank[3]]
        ps_flag = bank[2]

        s_x = [sem(f"x_in{yh}") for yh in range(YH)]
        s_cst = sem("const_in")
        s_win = sem("weights_in")
        s_prm = sem("params_in")
        s_late = sem("late_weights_in")
        s_zero = sem("memsets_done")
        s_off = sem("offsets_ready")
        s_log = sem("logits_ready")
        s_v = sem("values_ready")
        s_vp = sem("values_stored")
        s_u = sem("positions_ready")
        s_abs = sem("abs_ready")
        s_hat = sem("hats_ready")
        s_exp = sem("exp_ready")
        s_max = sem("max_ready")
        s_sub = sem("sub_ready")
        s_sum = sem("sums_ready")
        s_rec = sem("recips_ready")
        s_prob = sem("probs_ready")
        s_att = sem("probs_turned")
        s_ay = sem("ay_ready")
        s_a = sem("tap_weights_ready")
        s_w = sem("spread_ready")
        s_p = sem("products_ready")
        s_s2 = sem("pair_sums_ready")
        s_s4 = sem("row_sums_ready")
        s_o = sem("projected")
        s_ov1 = sem("over_abs")
        s_ov = sem("over_ready")
        s_last = sem("last_pair_sums_ready")
        s_fps = sem("flag_summed")
        s_f1 = sem("flag_steps")
        s_flag = sem("flag_ready")
        s_x1 = sem("x1_ready")
        s_sg = sem("signs_ready")
        s_wc = sem("conv_weights_ready")
        s_wab = sem("abs_weights_ready")
        s_pre = sem("bn_constants")
        s_y = sem("conv_ready")
        s_bns = sem("bn_stats_done")
        s_mv = sem("bn_aggregated")
        s_pair = sem("bn_paired")
        s_st = sem("bn_steps")
        s_sd = sem("bn_root")
        s_k = sem("bn_scale_ready")
        s_z = sem("z_ready")
        s_r = sem("relu_ready")
        s_q = sem("line_ready")
        s_res = sem("result_ready")
        s_done = sem("stored")
        s_ga = sem("g_weights_ready")
        s_gw = sem("g_spread_ready")
        s_gt = sem("g_probs_turned")
        s_gd = sem("g_steps")
        s_gc = sem("g_accumulated")
        s_go = sem("g_projected")
        s_gx = sem("g_x1_ready")
        s_gs = sem("g_signs_ready")

        def chunk(t, g, yh):
            return t[:, g, yh * HALF:(yh + 1) * HALF]

        def rows(ap):
            return ap.rearrange("p (y x) -> p y x", x=W)

        def along(ap, d):
            n = ap.shape[1]
            return ap.unsqueeze(1).to_broadcast([P, RH, n]) if d == 0 else ap.unsqueeze(2).to_broadcast([P, n, W])

        def sel_of(g):
            return cst[g * C:(g + 1) * C, c_sel:c_sel + P]

        def v_window(g, yh, ky, kx):
            y0 = yh * RH + ky + yh
            r = vpad[:, g, y0:y0 + RH, kx:kx + W + 1]
            return bass.AP(r.tensor, r.offset, [r.ap[0], [VP, RH], [W // 2 + 1, 2], [1, W // 2]])

        def by_col_half(ap):
            return ap.rearrange("p (y a x) -> p y a x", a=2, x=W // 2)

        block = ctx.enter_context(nc.Block())

        @block.sync
        def _(sp):
            for yh in range(YH):
                for g in range(G):
                    src = x[PAIR * g:PAIR * (g + 1)].rearrange("b c h w -> (b c) (h w)")
                    sp.dma_start(chunk(xs, g, yh), src[:, yh * HALF:(yh + 1) * HALF]).then_inc(s_x[yh], 16)
                if yh == 0:
                    sp.dma_start(cst[:], const).then_inc(s_cst, 16)
            sp.dma_start(wo[:], w_out).then_inc(s_late, 16)
            sp.dma_start(wcf[:], w_conv).then_inc(s_late, 16)
            sp.dma_start(wab[:], w_abs).then_inc(s_late, 16)
            n = 0
            for yh in range(YH):
                for g in range(G):
                    n += 1
                    sp.wait_ge(s_res, n)
                    dst = out[PAIR * g:PAIR * (g + 1)].rearrange("b c h w -> (b c) (h w)")
                    sp.dma_start(dst[:, yh * HALF:(yh + 1) * HALF], chunk(res, g, yh)).then_inc(s_done, 16)
            sp.wait_ge(s_done, 16 * G * YH)

        @block.tensor
        def _(pe):
            def offsets(yh):
                for d in range(2):
                    for g in range(G):
                        mm = pe.matmul(ps_off[yh][d][g * C:(g + 1) * C, :], wp[:, d, :], chunk(xs, g, yh), start=True, stop=True)
                    mm.then_inc(s_off, 1)

            def logits_bias(yh):
                pe.matmul(ps_log[yh][:], ones[0:1, :], prm[0:1, p_att:p_att + HP].unsqueeze(1).to_broadcast([1, HALF // HP, HP]),
                          start=True, stop=False, skip_group_check=True)

            def logits(yh):
                for n in range(NCH):
                    for g in range(G):
                        at = n * P + g * C
                        q = yh * HALF + n * P
                        mm = pe.matmul(ps_log[yh][:, at:at + C], xs[:, g, q:q + P], wp[:, 2, :], start=False,
                                       stop=(n == NCH - 1 and g == G - 1), skip_group_check=True)
                mm.then_inc(s_log, 1)

            def turn(yh):
                pe.wait_ge(s_prob, yh + 1)
                for n in range(NCH):
                    mm = pe.transpose(ps_att[yh][:, n * P:(n + 1) * P], prob[:, yh, n * P:(n + 1) * P], cst[:, c_eye:c_eye + P])
                mm.then_inc(s_att, 1)

            def spread(t):
                pe.wait_ge(s_a, t + 1)
                for g in range(G):
                    if t >= 2:
                        pe.wait_ge(s_p, 2 * (t - 2) + g + 1)
                    pe.matmul(ps_w[t % 2][g][:], sel_of(g), a[g * C:(g + 1) * C, t % AR, :], start=True, stop=True).then_inc(s_w, 1)

            def project(m):
                yh, ky = divmod(m, TAPS)
                pe.wait_ge(s_s4, m + 1)
                if m == 0:
                    pe.wait_ge(s_late, 48)
                    pe.wait_ge(s_ay, TAPS)
                if m == TAPS:
                    pe.wait_ge(s_ay, 2 * TAPS)
                    pe.wait_ge(s_f1, 1)
                for g in range(G):
                    mm = pe.matmul(ps_out[yh][g][:], wo[:], sum4[:, m % 2, g, :], start=(ky == 0), stop=(ky == TAPS - 1))
                mm.then_inc(s_o, 1)

            def project_last():
                for j in range(2):
                    for g in range(G):
                        pe.wait_ge(s_last, G * j + g + 1)
                        mm = pe.matmul(ps_out[1][g][:], wo[:], sum2[:, 1, j, g, :], start=False, stop=(j == 1))
                        if j == 1:
                            mm.then_inc(s_o, 1)

            pe.wait_ge(s_zero, 1)
            for n in range(3):
                pe.matmul(bank[5][:], ones[:], ones[:].unsqueeze(1).to_broadcast([P, HALF // P, P]), start=True, stop=True)
            pe.wait_ge(s_prm, 16)
            logits_bias(0)
            logits_bias(1)
            pe.wait_ge(s_win, 16)
            pe.wait_ge(s_x[0], 32)
            logits(0)
            offsets(0)
            pe.wait_ge(s_x[1], 32)
            for yh in range(YH):
                for g in range(G):
                    pe.matmul(ps_v[yh][g][:], wv, chunk(xs, g, yh), start=True, stop=True).then_inc(s_v, 1)
            logits(1)
            pe.wait_ge(s_cst, 16)
            pe.wait_ge(s_vp, 4)
            turn(0)
            for t in range(NT * YH):
                if t == 0:
                    pe.wait_ge(s_u, 2)
                if t == 1:
                    pe.wait_ge(s_sub, 2)
                spread(t)
                if t == 1:
                    offsets(1)
                if t == 8:
                    pe.wait_ge(s_u, 4)
                    turn(1)
                if t == 12:
                    pe.wait_ge(s_ov, 4)
                    pe.matmul(ps_flag[0:1, 0:4], ones[:, 0:1], over[:], start=True, stop=True).then_inc(s_fps, 1)
                if t % TAPS == TAPS - 1 and t > TAPS:
                    project(t // TAPS - 1)
            project_last()

            pe.wait_ge(s_flag, 1)
            beyond = pe.value_load(flagi[0:1, 0:1], min_val=0, max_val=1)
            with pe.If(beyond > 0):
                pe.wait_ge(s_x1, 4)
                for n in range(2 * NCH):
                    mm = pe.transpose(bank[n // NCH][:, (n % NCH) * P:(n % NCH + 1) * P],
                                      prob[:, n // NCH, (n % NCH) * P:(n % NCH + 1) * P], cst[:, c_eye:c_eye + P])
                mm.then_inc(s_gt, 1)
                with pe.Fori(0, NQ) as key:
                    pe.wait_ge(s_ga, key + 1)
                    for g in range(G):
                        for yh in range(YH):
                            mm = pe.matmul(bank[4 + 2 * yh + g][:], sel_of(g), ga[g * C:(g + 1) * C, yh * HALF:(yh + 1) * HALF],
                                           start=True, stop=True)
                    mm.then_inc(s_gw, 1)
                pe.wait_ge(s_gc, 1)
                for yh in range(YH):
                    for g in range(G):
                        mm = pe.matmul(ps_out[yh][g][:], wo[:], chunk(gacc, g, yh), start=True, stop=True)
                mm.then_inc(s_go, 1)
                pe.wait_ge(s_gs, 4)
            pe.end_ifs()

            pe.wait_ge(s_wc, 2)
            pe.wait_ge(s_p, 2 * NT * YH)
            for g in range(G):
                pe.wait_ge(s_sg, 3 + g)
                for yh in range(YH):
                    for k in range(K * K):
                        y0, x0 = yh * RH + k // K, k % K
                        mm = pe.matmul(ps_y[yh][g][:], wcb[:, k, :], sg[:, g, y0:y0 + RH, x0:x0 + W],
                                       start=(k == 0), stop=(k == K * K - 1))
                    mm.then_inc(s_y, 1)
            pe.wait_ge(s_mv, 1)
            pe.matmul(bank[0][:, 0:2], cst[:, c_avg:c_avg + P], mv[:, 0:2], start=True, stop=True)
            pe.matmul(bank[0][:, 2:3], cst[:, c_dif:c_dif + P], mv[:, 0:1], start=True, stop=True,
                      skip_group_check=True).then_inc(s_pair, 1)

        @block.scalar
        def _(act):
            act.dma_start(win[:], w_in).then_inc(s_win, 16)
            act.dma_start(prm[:], params).then_inc(s_prm, 16)

            order = [(0, 0, 0), (0, 1, 0), (0, 0, 1), (0, 0, 2), (0, 0, 3), (0, 1, 1), (0, 1, 2), (0, 1, 3)]
            order += [(1, d, k) for d in range(2) for k in range(TAPS)]

            def distance(n):
                yh, d, k = order[n]
                act.wait_ge(s_u, 2 * yh + d + 1)
                if n >= 3:
                    act.wait_ge(s_hat, n - 2)
                nc.scalar.activation(tab[:, n % 3, :], u[:, d, yh, :], ACT.Abs, bias=cst[:, c_tap + k:c_tap + k + 1]).then_inc(s_abs, 1)

            def hats(first, last):
                distance(first)
                for n in range(first, last):
                    if n + 1 < last:
                        distance(n + 1)
                    yh, d, k = order[n]
                    act.wait_ge(s_abs, n + 1)
                    nc.scalar.activation(hat[:, yh, d * TAPS + k, :], tab[:, n % 3, :], ACT.Relu, bias=1.0, scale=-1.0).then_inc(s_hat, 1)

            act.wait_ge(s_sub, 1)
            nc.scalar.activation(ex[:, 0, :], lsub[:, 0, :], ACT.Exp).then_inc(s_exp, 1)
            act.wait_ge(s_cst, 16)
            hats(0, 2)
            act.wait_ge(s_prm, 16)
            act.wait_ge(s_zero, 2)
            for n in range(G * YH):
                yh, g = divmod(n, G)
                act.wait_ge(s_v, n + 1)
                y0 = yh * RH - TAP0
                nc.scalar.activation(vpad[:, g, y0:y0 + RH, -TAP0:W - TAP0], rows(ps_v[yh][g][:]), ACT.Identity,
                                     bias=prm[:, p_bv:p_bv + 1]).then_inc(s_vp, 1)
            hats(2, 8)
            act.wait_ge(s_sub, 2)
            nc.scalar.activation(ex[:, 1, :], lsub[:, 1, :], ACT.Exp).then_inc(s_exp, 1)
            hats(8, 16)
            for n in range(2 * YH):
                yh, d = divmod(n, 2)
                if n >= 2:
                    act.wait_ge(s_ov, n - 1)
                nc.scalar.activation(overt[:, n % 2, :], u[:, d, yh, :], ACT.Abs, bias=cst[:, c_mid:c_mid + 1]).then_inc(s_ov1, 1)
                act.wait_ge(s_ov1, n + 1)
                nc.scalar.activation(overs[:, n % 2, :], overt[:, n % 2, :], ACT.Relu, bias=cst[:, c_mid + 1:c_mid + 2],
                                     accum_out=over[:, n:n + 1]).then_inc(s_ov, 1)
            act.wait_ge(s_late, 48)
            act.wait_ge(s_zero, 3)
            for i in range(PAIR):
                at = slice(i * C, (i + 1) * C)
                nc.scalar.activation(wcb[at, :, at], wcf[at, :].rearrange("p (k c) -> p k c", k=K * K), ACT.Sign).then_inc(s_wc, 1)
            nc.scalar.activation(wabs[:], wab[:], ACT.Abs, accum_out=st[:, 0:1]).then_inc(s_wab, 1)
            act.wait_ge(s_zero, 4)
            act.wait_ge(s_wab, 1)

            def signs(wait_on, done):
                for n in range(G * YH):
                    yh, g = divmod(n, G)
                    act.wait_ge(wait_on, n + 1)
                    nc.scalar.activation(sg[:, g, 1 + yh * RH:1 + (yh + 1) * RH, 1:1 + W], rows(chunk(x1, g, yh)), ACT.Sign,
                                         bias=prm[:, p_move0:p_move0 + 1]).then_inc(done, 1)

            signs(s_x1, s_sg)
            act.wait_ge(s_flag, 1)
            beyond = act.value_load(flagi[0:1, 0:1], min_val=0, max_val=1)
            with act.If(beyond > 0):
                signs(s_gx, s_gs)
            act.end_ifs()
            nc.scalar.activation(st[:, 14:15], ones[:, 0:1], ACT.Sqrt)
            act.wait_ge(s_st, 3)
            nc.scalar.activation(st[:, 8:9], st[:, 7:8], ACT.Sqrt).then_inc(s_sd, 1)
            act.wait_ge(s_k, 3)
            for n in range(G * YH):
                yh, g = divmod(n, G)
                act.wait_ge(s_z, n + 1)
                nc.scalar.activation(chunk(zr, g, yh), chunk(zz, g, yh), ACT.Relu, bias=st[:, 12:13]).then_inc(s_r, 1)
                nc.scalar.activation(chunk(zq, g, yh), chunk(zz, g, yh), ACT.Identity, bias=st[:, 13:14],
                                     scale=prm[:, p_prelu:p_prelu + 1]).then_inc(s_q, 1)

        @block.gpsimd
        def _(pool):
            pool.memset(ones[:], 1.0).then_inc(s_zero, 1)
            pool.memset(vpad[:].rearrange("p g y x -> p (g y x)"), 0.0).then_inc(s_zero, 1)
            pool.memset(wcb[:].rearrange("p k c -> p (k c)"), 0.0).then_inc(s_zero, 1)
            pool.memset(sg[:].rearrange("p g y x -> p (g y x)"), 0.0).then_inc(s_zero, 1)
            for m in range(TAPS * YH - 1):
                for j in range(2):
                    t = TAPS * m + 2 * j
                    pool.wait_ge(s_p, 2 * (t + 2))
                    if m >= 2:
                        pool.wait_ge(s_s4, m - 1)
                    pool.tensor_tensor(sum2[:, m % 2, j], prod[:, t % PR], prod[:, (t + 1) % PR], ALU.add).then_inc(s_s2, 1)
                pool.wait_ge(s_s2, 2 * m + 2)
                if m >= 2:
                    pool.wait_ge(s_o, m - 1)
                pool.tensor_tensor(sum4[:, m % 2], sum2[:, m % 2, 0], sum2[:, m % 2, 1], ALU.add).then_inc(s_s4, 1)

        @block.vector
        def _(dve):
            def positions(yh):
                for d in range(2):
                    n = 2 * yh + d
                    dve.wait_ge(s_off, n + 1)
                    at = cst[:, c_pos:c_pos + W] if d == 0 else cst[:, c_pos + yh * RH:c_pos + (yh + 1) * RH]
                    nc.vector.scalar_tensor_tensor(out=rows(u[:, d, yh, :]), in0=rows(ps_off[yh][d][:]), scalar=prm[:, p_off + d:p_off + d + 1],
                                                   in1=along(at, d), op0=ALU.add, op1=ALU.add).then_inc(s_u, 1)

            def grouped(ap):
                return ap.rearrange("p (n k) -> p n k", k=POINTS)

            def spread_points(ap):
                return ap.unsqueeze(2).to_broadcast([P, HALF // POINTS, POINTS])

            def softmax_head(yh):
                dve.wait_ge(s_log, yh + 1)
                nc.vector.tensor_reduce(lmax[:, yh, :], grouped(ps_log[yh][:]), AX.X, ALU.max).then_inc(s_max, 1)
                dve.wait_ge(s_max, yh + 1)
                nc.vector.tensor_tensor(grouped(lsub[:, yh, :]), grouped(ps_log[yh][:]), spread_points(lmax[:, yh, :]),
                                        ALU.subtract).then_inc(s_sub, 1)

            def softmax_tail(yh):
                dve.wait_ge(s_exp, yh + 1)
                nc.vector.tensor_reduce(lsum[:, yh, :], grouped(ex[:, yh, :]), AX.X, ALU.add).then_inc(s_sum, 1)
                dve.wait_ge(s_sum, yh + 1)
                nc.vector.reciprocal(lrec[:, yh, :], lsum[:, yh, :]).then_inc(s_rec, 1)
                dve.wait_ge(s_rec, yh + 1)
                nc.vector.tensor_tensor(grouped(prob[:, yh, :]), grouped(ex[:, yh, :]), spread_points(lrec[:, yh, :]),
                                        ALU.mult).then_inc(s_prob, 1)

            def attend(yh, ky):
                dve.wait_ge(s_att, yh + 1)
                dve.wait_ge(s_hat, (2 if ky == 0 else 5 + ky) if yh == 0 else 13 + ky)
                nc.vector.tensor_tensor(ay[:, yh, ky, :], ps_att[yh][:], hat[:, yh, TAPS + ky, :], ALU.mult).then_inc(s_ay, 1)

            def weight(t):
                yh, k = divmod(t, NT)
                ky, kx = divmod(k, TAPS)
                dve.wait_ge(s_ay, yh * TAPS + ky + 1)
                dve.wait_ge(s_hat, (1 if kx == 0 else 2 + kx) if yh == 0 else 9 + kx)
                if t >= AR:
                    dve.wait_ge(s_w, 2 * (t - AR + 1))
                nc.vector.tensor_tensor(a[:, t % AR, :], ay[:, yh, ky, :], hat[:, yh, kx, :], ALU.mult).then_inc(s_a, 1)

            def product(t):
                yh, k = divmod(t, NT)
                ky, kx = divmod(k, TAPS)
                if t == 0:
                    dve.wait_ge(s_vp, 4)
                if t >= PR:
                    dve.wait_ge(s_s2, (t - PR) // 2 + 1)
                for g in range(G):
                    dve.wait_ge(s_w, 2 * t + g + 1)
                    nc.vector.tensor_tensor(by_col_half(prod[:, t % PR, g, :]), by_col_half(ps_w[t % 2][g][:]),
                                            v_window(g, yh, ky, kx), ALU.mult).then_inc(s_p, 1)

            def residual_of(yh, g, done):
                nc.vector.scalar_tensor_tensor(out=chunk(x1, g, yh), in0=ps_out[yh][g][:], scalar=prm[:, p_bo:p_bo + 1],
                                               in1=chunk(xs, g, yh), op0=ALU.add, op1=ALU.add).then_inc(done, 1)

            def residual(yh, done):
                for g in range(G):
                    residual_of(yh, g, done)

            def last_pair(j):
                m = TAPS * YH - 1
                dve.wait_ge(s_s4, m - 1)
                for g in range(G):
                    t = TAPS * m + 2 * j
                    dve.wait_ge(s_p, 2 * (t + 1) + g + 1)
                    nc.vector.tensor_tensor(sum2[:, 1, j, g, :], prod[:, t % PR, g, :], prod[:, (t + 1) % PR, g, :],
                                            ALU.add).then_inc(s_last, 1)

            softmax_head(0)
            dve.wait_ge(s_cst, 16)
            dve.wait_ge(s_prm, 16)
            positions(0)
            softmax_tail(0)
            softmax_head(1)
            attend(0, 0)
            weight(0)
            weight(1)
            for ky in range(1, TAPS):
                attend(0, ky)
            for t in range(NT * YH):
                if t == 2:
                    positions(1)
                if t == 5:
                    softmax_tail(1)
                if 10 <= t < 10 + TAPS:
                    attend(1, t - 10)
                if t == 14:
                    dve.wait_ge(s_fps, 1)
                    nc.vector.reduce_sum(flag[:, 0:1], ps_flag[0:1, 0:4], AX.X).then_inc(s_f1, 1)
                if t == 16:
                    dve.wait_ge(s_f1, 1)
                    nc.vector.tensor_scalar(flagi[:], flag[:, 0:1], 0.0, None, ALU.is_gt).then_inc(s_flag, 1)
                if t == 18:
                    dve.wait_ge(s_wab, 1)
                    nc.vector.tensor_scalar(st[:, 1:2], st[:, 0:1], 1.0 / (K * K * C), None, ALU.mult).then_inc(s_pre, 1)
                    nc.vector.tensor_tensor(st[:, 4:5], prm[:, p_beta:p_beta + 1], prm[:, p_move1:p_move1 + 1], ALU.add).then_inc(s_pre, 1)
                    nc.vector.tensor_scalar(st[:, 5:6], prm[:, p_prelu:p_prelu + 1], -1.0, 1.0, ALU.mult, ALU.add).then_inc(s_pre, 1)
                    dve.wait_ge(s_pre, 3)
                    nc.vector.tensor_tensor(st[:, 2:3], st[:, 1:2], st[:, 1:2], ALU.mult).then_inc(s_pre, 1)
                    nc.vector.tensor_tensor(st[:, 3:4], st[:, 1:2], prm[:, p_gamma:p_gamma + 1], ALU.mult).then_inc(s_pre, 1)
                if t + 2 < NT * YH:
                    weight(t + 2)
                product(t)
                if t == NT + 8:
                    dve.wait_ge(s_o, TAPS)
                    residual(0, s_x1)
                if t == NT * YH - 2:
                    last_pair(0)
            last_pair(1)
            for g in range(G):
                dve.wait_ge(s_o, TAPS * YH - 1 + g + 1)
                residual_of(1, g, s_x1)

            beyond = dve.value_load(flagi[0:1, 0:1], min_val=0, max_val=1)
            with dve.If(beyond > 0):
                dve.wait_ge(s_gt, 1)
                for yh in range(YH):
                    nc.vector.tensor_copy(gatt[:, yh * HALF:(yh + 1) * HALF], bank[yh][:]).then_inc(s_gd, 1)
                    for d in range(2):
                        at = cst[:, c_abs:c_abs + W] if d == 0 else cst[:, c_abs + yh * RH:c_abs + (yh + 1) * RH]
                        nc.vector.tensor_tensor(rows(gxy[:, d, yh * HALF:(yh + 1) * HALF]), rows(u[:, d, yh, :]), along(at, d),
                                                ALU.add).then_inc(s_gd, 1)
                nc.vector.memset(gacc[:].rearrange("p g n -> p (g n)"), 0.0).then_inc(s_gd, 1)

                def general_hat(axis, key, times, into, base, done):
                    dve.wait_ge(s_gd, base)
                    nc.vector.tensor_scalar(gt[:, 0, :], gxy[:, axis, :], cst[:, bass.ds(c_neg + key, 1)], 1.0, ALU.add,
                                            ALU.add).then_inc(s_gd, 1)
                    dve.wait_ge(s_gd, base + 1)
                    nc.vector.tensor_scalar(gt[:, 1, :], gt[:, 0, :], -1.0, 2.0, ALU.mult, ALU.add).then_inc(s_gd, 1)
                    dve.wait_ge(s_gd, base + 2)
                    nc.vector.tensor_tensor(gt[:, 0, :], gt[:, 0, :], gt[:, 1, :], ALU.min).then_inc(s_gd, 1)
                    dve.wait_ge(s_gd, base + 3)
                    nc.vector.scalar_tensor_tensor(out=into, in0=gt[:, 0, :], scalar=0.0, in1=times, op0=ALU.max,
                                                   op1=ALU.mult).then_inc(done, 1)

                SETUP, PER_Y, PER_X = 7, 4, 3 + G * YH
                with dve.Fori(0, H) as key_y:
                    at_y = SETUP + key_y * (PER_Y + PER_X * W)
                    general_hat(1, key_y, gatt, gay, at_y, s_gd)
                    with dve.Fori(0, W) as key_x:
                        at_x = at_y + PER_Y + PER_X * key_x
                        general_hat(0, key_x, gay, ga, at_x, s_ga)
                        dve.wait_ge(s_gw, W * key_y + key_x + 1)
                        for g in range(G):
                            value = vpad[:, g].rearrange("p y x -> p (y x)")[
                                :, bass.ds(key_y * VP + key_x + (VP + 1) * -TAP0, 1)]
                            for yh in range(YH):
                                nc.vector.scalar_tensor_tensor(out=chunk(gacc, g, yh), in0=bank[4 + 2 * yh + g][:], scalar=value,
                                                               in1=chunk(gacc, g, yh), op0=ALU.mult, op1=ALU.add).then_inc(s_gd, 1)
                dve.wait_ge(s_gd, SETUP + H * (PER_Y + PER_X * W))
                dve.sem_inc(s_gc, 1)
                dve.wait_ge(s_go, 1)
                dve.wait_ge(s_sg, 4)
                for yh in range(YH):
                    residual(yh, s_gx)
            dve.end_ifs()

            for n in range(G * YH):
                g, yh = divmod(n, YH)
                dve.wait_ge(s_y, n + 1)
                nc.vector.bn_stats(bns[:, n, :], ps_y[yh][g][:]).then_inc(s_bns, 1)
            dve.wait_ge(s_bns, G * YH)
            nc.vector.bn_aggr(mv[:], bns[:].rearrange("p n s -> p (n s)")).then_inc(s_mv, 1)
            dve.wait_ge(s_pair, 1)
            nc.vector.tensor_copy(st[:, 9:12], bank[0][:, 0:3]).then_inc(s_st, 1)
            dve.wait_ge(s_st, 1)
            dve.wait_ge(s_pre, 5)
            nc.vector.scalar_tensor_tensor(out=st[:, 6:7], in0=st[:, 11:12], scalar=st[:, 11:12], in1=st[:, 10:11], op0=ALU.mult,
                                           op1=ALU.add).then_inc(s_st, 1)
            dve.wait_ge(s_st, 2)
            nc.vector.tensor_scalar(st[:, 7:8], st[:, 6:7], st[:, 2:3], BN_EPS, ALU.mult, ALU.add).then_inc(s_st, 1)
            dve.wait_ge(s_sd, 1)
            nc.vector.reciprocal(st[:, 6:7], st[:, 8:9]).then_inc(s_st, 1)
            dve.wait_ge(s_st, 4)
            nc.vector.scalar_tensor_tensor(out=st[:, 8:9], in0=st[:, 6:7], scalar=st[:, 6:7], in1=st[:, 7:8], op0=ALU.mult,
                                           op1=ALU.mult).then_inc(s_st, 1)
            dve.wait_ge(s_st, 5)
            nc.vector.tensor_scalar(st[:, 11:12], st[:, 8:9], -0.5, 1.5, ALU.mult, ALU.add).then_inc(s_st, 1)
            dve.wait_ge(s_st, 6)
            nc.vector.scalar_tensor_tensor(out=st[:, 10:11], in0=st[:, 11:12], scalar=st[:, 6:7], in1=st[:, 3:4], op0=ALU.mult,
                                           op1=ALU.mult).then_inc(s_k, 1)
            dve.wait_ge(s_k, 1)
            nc.vector.scalar_tensor_tensor(out=st[:, 12:13], in0=st[:, 9:10], scalar=st[:, 10:11], in1=st[:, 4:5], op0=ALU.mult,
                                           op1=ALU.subtract, reverse1=True).then_inc(s_k, 1)
            dve.wait_ge(s_k, 2)
            nc.vector.tensor_scalar(st[:, 13:14], st[:, 12:13], prm[:, p_prelu:p_prelu + 1], prm[:, p_move2:p_move2 + 1], ALU.mult, ALU.add).then_inc(s_k, 1)

            def scaled(n):
                yh, g = divmod(n, G)
                nc.vector.scalar_tensor_tensor(out=chunk(zz, g, yh), in0=ps_y[yh][g][:], scalar=st[:, 10:11], in1=chunk(x1, g, yh),
                                               op0=ALU.mult, op1=ALU.add).then_inc(s_z, 1)

            def prelu(n):
                yh, g = divmod(n, G)
                dve.wait_ge(s_r, n + 1)
                dve.wait_ge(s_q, n + 1)
                nc.vector.scalar_tensor_tensor(out=chunk(res, g, yh), in0=chunk(zr, g, yh), scalar=st[:, 5:6], in1=chunk(zq, g, yh),
                                               op0=ALU.mult, op1=ALU.add).then_inc(s_res, 1)

            for n in range(G * YH):
                scaled(n)
                if n >= 2:
                    prelu(n - 2)
            prelu(2)
            prelu(3)


def kernel(**inputs):
    import concourse.bacc as _bacc
    from concourse.bass_utils import run_bass_kernel_spmd as _run

    def get(name):
        return np.ascontiguousarray(inputs[name])

    def blocks(w):
        out = np.zeros((P, w.shape[1] * PAIR), w.dtype)
        for i in range(PAIR):
            out[i * w.shape[0]:(i + 1) * w.shape[0], i * w.shape[1]:(i + 1) * w.shape[1]] = w
        return out

    w_off = get("L0_conv_W_off").reshape(C, HP, 2)
    w_proj = np.stack([blocks(w_off[:, :, 0]), blocks(w_off[:, :, 1]), blocks(get("L0_conv_W_attn"))], 1)
    conv_w = get("L1_conv_conv_w")
    params = [get(n).reshape(C) for n in ("L0_conv_b_value", "L0_conv_b_out", "L1_conv_move0_bias", "L1_conv_bn_gamma",
                                          "L1_conv_bn_beta", "L1_conv_move1_bias", "L1_conv_prelu_a", "L1_conv_move2_bias")]
    arrays = {
        "x": get("x"),
        "const": constants(),
        "w_in": np.concatenate([w_proj.reshape(P, -1), blocks(get("L0_conv_W_value"))], 1),
        "w_out": blocks(get("L0_conv_W_out")),
        "params": np.concatenate([np.tile(np.stack(params, 1), (PAIR, 1)), np.tile(get("L0_conv_b_off").reshape(HP, 2), (B, 1)),
                                  np.tile(get("L0_conv_b_attn").reshape(1, HP), (P, 1))], 1),
        "w_conv": np.tile(conv_w.transpose(1, 2, 3, 0).reshape(C, K * K * C), (PAIR, 1)),
        "w_abs": np.tile(conv_w.reshape(C, C * K * K), (PAIR, 1)),
    }
    arrays = {n + "_dram": np.ascontiguousarray(v) for n, v in arrays.items()}
    nc = _bacc.Bacc("TRN2", target_bir_lowering=False, num_devices=1)
    args = [nc.dram_tensor(n, v.shape, F32, kind="ExternalInput").ap() for n, v in arrays.items()]
    args.append(nc.dram_tensor("out_dram", (B, C, H, W), F32, kind="ExternalOutput").ap())
    deformable_attention_then_binary_conv(nc, *args)
    r = _run(nc, [arrays], core_ids=[0])
    return r.results[0]["out_dram"]
```

```python
from contextlib import ExitStack

import numpy as np

import concourse.bass as bass
from concourse import mybir

F32 = mybir.dt.float32
BF16 = mybir.dt.bfloat16
I32 = mybir.dt.int32
ALU = mybir.AluOpType
ACT = mybir.ActivationFunctionType
AX = mybir.AxisListType

B, C, H, W = 4, 64, 32, 32
HEADS, POINTS = 8, 4
HD = C // HEADS
HP = HEADS * POINTS
NQ = H * W
PAIR = 2
G = B // PAIR
P = PAIR * C
YH = 2
RH = H // YH
HALF = RH * W
NCH = HALF // P
TAPS = 4
NT = TAPS * TAPS
TAP0 = -2
GPSIMD_ROWS = (0, 1, 2)
GPSIMD_PAIRS = (0, 1)
GPSIMD_LINES = (0, 1)
PROJECT_AT = (18, 25, 30)
VP = H + TAPS
HW = W // 2
SEG = HW + TAPS - 1
CP = W + 2
K = 3
BN_EPS = 1e-5
p_bv, p_bo, p_move0, p_gamma, p_beta, p_move1, p_prelu, p_move2 = range(8)
p_off = 8
p_att = p_off + 2
NPRM = p_att + HP


def constants():
    j = np.arange(W)
    second = (j >= W // 2).astype(np.float64)
    pos = np.linspace(0.0, 1.0, W) * W - 0.5 - j - second
    sel = np.zeros((P, G, P), np.float32)
    for g in range(G):
        for i in range(PAIR):
            for h in range(HEADS):
                row = g * C + i * HP + h * POINTS
                sel[row:row + POINTS, g, i * C + h * HD:i * C + (h + 1) * HD] = 1.0
    eye = np.eye(C)
    avg = np.block([[eye, eye], [eye, eye]]) * 0.5
    diff = np.block([[eye, -eye], [-eye, eye]]) * 0.5
    rows = [pos, j + second, -j, [-(TAP0 + k) for k in range(TAPS)], [0.5, -1.5]]
    rows = np.tile(np.concatenate(rows)[None], (P, 1))
    return np.concatenate([rows, sel.reshape(P, G * P), np.eye(P), avg, diff], 1).astype(np.float32)


c_pos, c_abs, c_neg = 0, W, 2 * W
c_tap = 3 * W
c_mid = c_tap + TAPS
c_sel = c_mid + 2
c_eye = c_sel + G * P
c_avg = c_eye + P
c_dif = c_avg + P
NCONST = c_dif + P


def deformable_attention_then_binary_conv(nc, x, const, w_in, w_out, params, w_conv, w_abs, out):
    ctx = ExitStack()
    with ctx:
        def sb(name, shape, dt=F32):
            return ctx.enter_context(nc.sbuf_tensor(name, shape, dt))

        def sem(name):
            return ctx.enter_context(nc.semaphore(name))

        xs = sb("xs", [P, G, NQ])
        cst = sb("cst", [P, NCONST])
        win = sb("win", [P, 3 * PAIR * HP + P])
        wp = win[:, 0:3 * PAIR * HP].rearrange("p (k n) -> p k n", k=3)
        wv = win[:, 3 * PAIR * HP:]
        wo = sb("wo", [P, P])
        ones = sb("ones", [P, P])
        top_ones = sb("top_ones", [P, P])
        prm = sb("prm", [P, NPRM])
        wcf = sb("wcf", [P, K * K * C])
        wab = sb("wab", [P, K * K * C])
        wcb = sb("wcb", [P, K * K, P], BF16)
        vpad = sb("vpad", [P, G, VP, 2, SEG])
        u = sb("u", [P, 2, YH, HALF])
        tab = sb("tab", [P, 3, HALF])
        hat = sb("hat", [P, 2, 2 * TAPS, HALF])
        ay = sb("ay", [P, 2, TAPS, HALF])
        lsub = sb("lsub", [P, YH, HALF])
        ex = sb("ex", [P, YH, HALF])
        prob = sb("prob", [P, YH, HALF])
        lmax = sb("lmax", [P, YH, HALF // POINTS])
        lsum = sb("lsum", [P, YH, HALF // POINTS])
        lrec = sb("lrec", [P, YH, HALF // POINTS])
        a = sb("a", [P, TAPS, HALF])
        PR = 8
        prod = sb("prod", [P, PR, G, HALF])
        sum2 = sb("sum2", [P, 2, 2, G, HALF])
        sum4 = sb("sum4", [P, 2, G, HALF])
        sum8 = sb("sum8", [P, G, HALF])
        over = sb("over", [P, 2 * YH])
        overt = sb("overt", [P, 2, HALF])
        overs = sb("overs", [P, 2, HALF])
        flag = sb("flag", [1, 2])
        flagi = sb("flagi", [1, 1], I32)
        x1 = sb("x1", [P, G, NQ])
        sg = sb("sg", [P, G, CP, CP], BF16)
        wabs = sb("wabs", [P, K * K * C])
        bns = sb("bns", [P, G * YH, 6])
        mv = sb("mv", [P, 2])
        st = sb("st", [P, 16])
        spare = prod[:].rearrange("p r g n -> p (r g n)")

        def share(i, n, of=spare):
            return of[:, i * NQ:(i + n) * NQ]

        zz, zr, zq, res = (share(2 * i, 2).rearrange("p (g n) -> p g n", g=G) for i in range(4))
        gxy = share(0, 2).rearrange("p (d n) -> p d n", d=2)
        gt = share(2, 2).rearrange("p (d n) -> p d n", d=2)
        gatt, gay, ga = share(4, 1), share(5, 1), share(6, 1)
        gacc = share(0, 2, sum2[:].rearrange("p m j g n -> p (m j g n)")).rearrange("p (g n) -> p g n", g=G)

        banks = [ctx.enter_context(nc.psum_tensor(f"banks{i}", [P, G, HALF], F32)) for i in range(4)]
        bank = [banks[i // 2][:, i % 2, :] for i in range(8)]
        ps_out = [[bank[0], bank[1]], [bank[2], bank[3]]]
        ps_w = [banks[2], banks[3]]
        ps_y = [[bank[0], bank[1]], [bank[6], bank[7]]]
        ps_v = [[bank[0], bank[1]], [bank[7], bank[3]]]
        ps_off = [[bank[4], bank[5]], [bank[0], bank[1]]]
        ps_log = [bank[6], bank[3]]
        ps_att = [bank[2], bank[3]]
        ps_flag = bank[2]

        s_x = [sem(f"x_in{yh}") for yh in range(YH)]
        s_cst = sem("const_in")
        s_win = sem("weights_in")
        s_prm = sem("params_in")
        s_late = sem("late_weights_in")
        s_zero = sem("memsets_done")
        s_top = sem("top_ones_set")
        s_off = sem("offsets_ready")
        s_log = sem("logits_ready")
        s_v = sem("values_ready")
        s_vp = sem("upper_values_stored")
        s_vlow = sem("lower_values_stored")
        s_u = sem("positions_ready")
        s_abs = sem("abs_ready")
        s_hat = sem("hats_ready")
        s_exp = sem("exp_ready")
        s_max = sem("max_ready")
        s_sub = sem("sub_ready")
        s_sum = sem("sums_ready")
        s_rec = sem("recips_ready")
        s_prob = sem("probs_ready")
        s_att = sem("probs_turned")
        s_ay = sem("ay_ready")
        s_a = sem("tap_weights_ready")
        s_ap = sem("gpsimd_tap_weights_ready")
        s_w = sem("spread_ready")
        s_p = sem("products_ready")
        s_s2 = sem("pair_sums_ready")
        s_s4 = sem("row_sums_ready")
        s_s8 = sem("two_rows_sums_ready")
        s_o = sem("projected")
        s_ov1 = sem("over_abs")
        s_ov = sem("over_ready")
        s_last = sem("last_pair_sums_ready")
        s_seven = sem("row_6_and_pair_ready")
        s_fps = sem("flag_summed")
        s_f1 = sem("flag_steps")
        s_flag = sem("flag_ready")
        s_x1 = sem("x1_ready")
        s_sg = sem("signs_ready")
        s_wc = sem("conv_weights_ready")
        s_wab = sem("abs_weights_ready")
        s_pre = sem("bn_constants")
        s_y = sem("conv_ready")
        s_bns = sem("bn_stats_done")
        s_mv = sem("bn_aggregated")
        s_pair = sem("bn_paired")
        s_st = sem("bn_steps")
        s_sd = sem("bn_root")
        s_k = sem("bn_scale_ready")
        s_shift = sem("bn_shift_steps")
        s_z = sem("z_ready")
        s_r = sem("relu_ready")
        s_q = sem("line_ready")
        s_l = sem("gpsimd_line_ready")
        s_res = sem("result_ready")
        s_done = sem("stored")
        s_ga = sem("g_weights_ready")
        s_gw = sem("g_spread_ready")
        s_gt = sem("g_probs_turned")
        s_gd = sem("g_steps")
        s_gc = sem("g_accumulated")
        s_go = sem("g_projected")
        s_gx = sem("g_x1_ready")
        s_gs = sem("g_signs_ready")

        def chunk(t, g, yh):
            return t[:, g, yh * HALF:(yh + 1) * HALF]

        def chunk_of(images, g, yh):
            src = images[PAIR * g:PAIR * (g + 1)].rearrange("b c h w -> (b c) (h w)")
            return src[:, yh * HALF:(yh + 1) * HALF]

        def rows(ap):
            return ap.rearrange("p (y x) -> p y x", x=W)

        def along(ap, d):
            n = ap.shape[1]
            return ap.unsqueeze(1).to_broadcast([P, RH, n]) if d == 0 else ap.unsqueeze(2).to_broadcast([P, n, W])

        def grouped(ap):
            return ap.rearrange("p (n k) -> p n k", k=POINTS)

        def spread_points(ap):
            return ap.unsqueeze(2).to_broadcast([P, HALF // POINTS, POINTS])

        def sel_of(g):
            return cst[:, c_sel + g * P:c_sel + (g + 1) * P]

        def v_window(g, yh, ky, kx):
            y0 = yh * RH + ky + yh
            return vpad[:, g, y0:y0 + RH, :, kx:kx + HW].rearrange("p g y a x -> p g (y a) x")

        def values_of(g, yh):
            y0 = yh * RH - TAP0
            r = vpad[:, g, y0:y0 + RH, 0, -TAP0:]
            return bass.AP(r.tensor, r.offset, [r.ap[0], [2 * SEG, RH], [SEG + TAP0, 2], [1, HW + 1]])

        def both_halves(ap):
            r = rows(ap)
            return bass.AP(r.tensor, r.offset, [r.ap[0], [W, RH], [HW - 1, 2], [1, HW + 1]])

        def by_half_row(ap):
            return ap.rearrange("p g (n x) -> p g n x", x=HW)

        def is_gpsimds(t):
            return t % TAPS == TAPS - 1 and t // TAPS in GPSIMD_ROWS

        def weights_done(t):
            return sum(is_gpsimds(n) == is_gpsimds(t) for n in range(t + 1))

        def products_done(t, g):
            n = NT * YH - 2
            return t + 1 if t < n else n + 2 * (t - n) + g + 1

        block = ctx.enter_context(nc.Block())

        @block.sync
        def _(sp):
            sp.dma_start(prm[:], params).then_inc(s_prm, 16)
            sp.dma_start(chunk(xs, 1, 0), chunk_of(x, 1, 0)).then_inc(s_x[0], 16)
            sp.dma_start(cst[:], const).then_inc(s_cst, 16)
            for g in range(G):
                sp.dma_start(chunk(xs, g, 1), chunk_of(x, g, 1)).then_inc(s_x[1], 16)
            sp.dma_start(wo[:], w_out).then_inc(s_late, 16)
            sp.dma_start(wcf[:], w_conv).then_inc(s_late, 16)
            sp.dma_start(wab[:], w_abs).then_inc(s_late, 16)
            for n in range(G * YH):
                yh, g = divmod(n, G)
                sp.wait_ge(s_res, n + 1)
                sp.dma_start(chunk_of(out, g, yh), chunk(res, g, yh)).then_inc(s_done, 16)
            sp.wait_ge(s_done, 16 * G * YH)

        @block.tensor
        def _(pe):
            def offsets(yh):
                for d in range(2):
                    for g in range(G):
                        mm = pe.matmul(ps_off[yh][d][g * C:(g + 1) * C, :], wp[:, d, :], chunk(xs, g, yh), start=True, stop=True)
                    mm.then_inc(s_off, 1)

            def logits_bias(yh):
                pe.matmul(ps_log[yh][:], top_ones[:], prm[:, p_att:p_att + HP].unsqueeze(1).to_broadcast([P, HALF // HP, HP]),
                          start=True, stop=False, skip_group_check=True)

            def logits(yh):
                for n in range(NCH):
                    for g in range(G):
                        at = n * P + g * C
                        q = yh * HALF + n * P
                        mm = pe.matmul(ps_log[yh][:, at:at + C], xs[:, g, q:q + P], wp[:, 2, :], start=False,
                                       stop=(n == NCH - 1 and g == G - 1), skip_group_check=True)
                mm.then_inc(s_log, 1)

            def values(yh):
                for g in range(G):
                    pe.matmul(ps_v[yh][g][:], wv, chunk(xs, g, yh), start=True, stop=True).then_inc(s_v, 1)

            def turn(yh):
                pe.wait_ge(s_prob, yh + 1)
                for n in range(NCH):
                    mm = pe.transpose(ps_att[yh][:, n * P:(n + 1) * P], prob[:, yh, n * P:(n + 1) * P], cst[:, c_eye:c_eye + P])
                mm.then_inc(s_att, 1)

            def spread(t):
                pe.wait_ge(s_ap if is_gpsimds(t) else s_a, weights_done(t))
                if t >= 2:
                    pe.wait_ge(s_p, products_done(t - 2, G - 1))
                for g in range(G):
                    pe.matmul(ps_w[t % 2][:, g, :], sel_of(g), a[:, t % TAPS, :], start=True, stop=True).then_inc(s_w, 1)

            def project_two_rows(j):
                yh = j // 2
                pe.wait_ge(s_s8, j + 1)
                if j == 0:
                    pe.wait_ge(s_late, 48)
                    pe.wait_ge(s_u, 2 * YH)
                if j == 2:
                    pe.wait_ge(s_ay, 2 * TAPS)
                    pe.wait_ge(s_f1, 1)
                for g in range(G):
                    mm = pe.matmul(ps_out[yh][g][:], wo[:], sum8[:, g, :], start=(j != 1), stop=(j == 1))
                mm.then_inc(s_o, 1)

            def project_last(j):
                for g in range(G):
                    if j == 0:
                        pe.wait_ge(s_seven, g + 1)
                        pe.matmul(ps_out[1][g][:], wo[:], sum4[:, 1, g, :], start=False, stop=False)
                    else:
                        pe.wait_ge(s_last, G + g + 1)
                        pe.matmul(ps_out[1][g][:], wo[:], sum2[:, 1, 1, g, :], start=False, stop=True).then_inc(s_o, 1)

            def convolve_row(yh, g, ky, first_row, last_row):
                for kx in range(K):
                    y0 = yh * RH + first_row + ky
                    mm = pe.matmul(ps_y[yh][g][:, first_row * W:last_row * W], wcb[:, ky * K + kx, :],
                                   sg[:, g, y0:y0 + last_row - first_row, kx:kx + W], start=(ky == 0 and kx == 0),
                                   stop=(ky == K - 1 and kx == K - 1 and last_row == RH), skip_group_check=True)
                return mm

            def convolve_above(g, ky):
                convolve_row(0, g, ky, 0, RH if ky < K - 1 else RH - 1)

            def convolve_rest(g):
                convolve_row(0, g, 2, RH - 1, RH).then_inc(s_y, 1)
                for ky in range(K):
                    mm = convolve_row(1, g, ky, 0, RH)
                mm.then_inc(s_y, 1)

            pe.wait_ge(s_zero, 1)
            for n in range(3):
                pe.matmul(bank[5][:, 0:2 * P], ones[:], ones[:].unsqueeze(1).to_broadcast([P, 2, P]), start=True, stop=True)
            pe.wait_ge(s_top, 2)
            pe.wait_ge(s_prm, 16)
            logits_bias(0)
            pe.wait_ge(s_win, 16)
            pe.wait_ge(s_x[0], 32)
            logits(0)
            offsets(0)
            pe.wait_ge(s_x[1], 32)
            values(0)
            pe.wait_ge(s_cst, 16)
            turn(0)
            values(1)
            for t in range(NT * YH):
                if t == 0:
                    pe.wait_ge(s_u, 2)
                if t == 1:
                    pe.wait_ge(s_sub, 1)
                    pe.wait_ge(s_vlow, 2)
                spread(t)
                if t == 2:
                    logits_bias(1)
                    logits(1)
                if t == 3:
                    pe.wait_ge(s_vp, 2)
                    offsets(1)
                if t == 11:
                    turn(1)
                if t == 14:
                    pe.wait_ge(s_ov, 4)
                    pe.wait_ge(s_ay, TAPS)
                    pe.matmul(ps_flag[0:1, 0:4], ones[:, 0:1], over[:], start=True, stop=True).then_inc(s_fps, 1)
                if t in PROJECT_AT:
                    project_two_rows(PROJECT_AT.index(t))
                if t == 29:
                    pe.wait_ge(s_wc, 2)
                    pe.wait_ge(s_sg, 2)
                    for ky in range(K):
                        convolve_above(0, ky)
            project_last(0)
            convolve_above(1, 0)
            project_last(1)
            convolve_above(1, 1)
            convolve_above(1, 2)

            pe.wait_ge(s_flag, 1)
            beyond = pe.value_load(flagi[0:1, 0:1], min_val=0, max_val=1)
            with pe.If(beyond > 0):
                pe.wait_ge(s_x1, 4)
                for n in range(2 * NCH):
                    mm = pe.transpose(bank[n // NCH][:, (n % NCH) * P:(n % NCH + 1) * P],
                                      prob[:, n // NCH, (n % NCH) * P:(n % NCH + 1) * P], cst[:, c_eye:c_eye + P])
                mm.then_inc(s_gt, 1)
                with pe.Fori(0, NQ) as key:
                    pe.wait_ge(s_ga, key + 1)
                    for g in range(G):
                        for yh in range(YH):
                            mm = pe.matmul(bank[4 + 2 * yh + g][:], sel_of(g), ga[:, yh * HALF:(yh + 1) * HALF],
                                           start=True, stop=True)
                    mm.then_inc(s_gw, 1)
                pe.wait_ge(s_gc, 1)
                for yh in range(YH):
                    for g in range(G):
                        mm = pe.matmul(ps_out[yh][g][:], wo[:], chunk(gacc, g, yh), start=True, stop=True)
                mm.then_inc(s_go, 1)
                pe.wait_ge(s_gs, 4)
                for g in range(G):
                    for ky in range(K):
                        convolve_above(g, ky)
            pe.end_ifs()

            pe.wait_ge(s_p, products_done(NT * YH - 1, G - 1))
            for g in range(G):
                pe.wait_ge(s_sg, 3 + g)
                convolve_rest(g)
            pe.wait_ge(s_mv, 1)
            pe.matmul(bank[4][:, 0:2], cst[:, c_avg:c_avg + P], mv[:, 0:2], start=True, stop=True)
            pe.matmul(bank[4][:, 2:3], cst[:, c_dif:c_dif + P], mv[:, 0:1], start=True, stop=True,
                      skip_group_check=True).then_inc(s_pair, 1)

        @block.scalar
        def _(act):
            act.dma_start(chunk(xs, 0, 0), chunk_of(x, 0, 0)).then_inc(s_x[0], 16)
            act.dma_start(win[:], w_in).then_inc(s_win, 16)

            order = [(0, 0, 0), (0, 1, 0), (0, 0, 1), (0, 0, 2), (0, 0, 3), (0, 1, 1), (0, 1, 2), (0, 1, 3)]
            order += [(1, d, k) for d in range(2) for k in range(TAPS)]

            def distance(n):
                yh, d, k = order[n]
                act.wait_ge(s_u, 2 * yh + d + 1)
                if n >= 3:
                    act.wait_ge(s_hat, n - 2)
                nc.scalar.activation(tab[:, n % 3, :], u[:, d, yh, :], ACT.Abs, bias=cst[:, c_tap + k:c_tap + k + 1]).then_inc(s_abs, 1)

            def hats(first, last):
                distance(first)
                for n in range(first, last):
                    if n + 1 < last:
                        distance(n + 1)
                    yh, d, k = order[n]
                    act.wait_ge(s_abs, n + 1)
                    nc.scalar.activation(hat[:, yh, d * TAPS + k, :], tab[:, n % 3, :], ACT.Relu, bias=1.0, scale=-1.0).then_inc(s_hat, 1)

            act.wait_ge(s_sub, 1)
            nc.scalar.activation(ex[:, 0, :], lsub[:, 0, :], ACT.Exp).then_inc(s_exp, 1)
            act.wait_ge(s_cst, 16)
            hats(0, 1)
            hats(1, 2)
            act.wait_ge(s_prm, 16)
            act.wait_ge(s_zero, 2)
            for g in range(G):
                act.wait_ge(s_v, g + 1)
                nc.scalar.activation(values_of(g, 0), both_halves(ps_v[0][g][:]), ACT.Identity,
                                     bias=prm[:, p_bv:p_bv + 1]).then_inc(s_vp, 1)
            hats(2, 8)
            act.wait_ge(s_sub, 2)
            nc.scalar.activation(ex[:, 1, :], lsub[:, 1, :], ACT.Exp).then_inc(s_exp, 1)
            hats(8, 16)
            for n in range(2 * YH):
                yh, d = divmod(n, 2)
                if n >= 2:
                    act.wait_ge(s_ov, n - 1)
                nc.scalar.activation(overt[:, n % 2, :], u[:, d, yh, :], ACT.Abs, bias=cst[:, c_mid:c_mid + 1]).then_inc(s_ov1, 1)
                act.wait_ge(s_ov1, n + 1)
                nc.scalar.activation(overs[:, n % 2, :], overt[:, n % 2, :], ACT.Relu, bias=cst[:, c_mid + 1:c_mid + 2],
                                     accum_out=over[:, n:n + 1]).then_inc(s_ov, 1)
            act.wait_ge(s_late, 48)
            act.wait_ge(s_zero, 3)
            for i in range(PAIR):
                at = slice(i * C, (i + 1) * C)
                nc.scalar.activation(wcb[at, :, at], wcf[at, :].rearrange("p (k c) -> p k c", k=K * K), ACT.Sign).then_inc(s_wc, 1)
            nc.scalar.activation(wabs[:], wab[:], ACT.Abs, accum_out=st[:, 0:1]).then_inc(s_wab, 1)
            act.wait_ge(s_wab, 1)
            nc.scalar.activation(st[:, 1:2], st[:, 0:1], ACT.Identity, scale=1.0 / (K * K * C)).then_inc(s_pre, 1)
            nc.scalar.activation(st[:, 4:5], prm[:, p_beta:p_beta + 1], ACT.Identity, bias=prm[:, p_move1:p_move1 + 1]).then_inc(s_pre, 1)
            nc.scalar.activation(st[:, 5:6], prm[:, p_prelu:p_prelu + 1], ACT.Identity, scale=-1.0, bias=1.0).then_inc(s_pre, 1)
            act.wait_ge(s_pre, 1)
            nc.scalar.activation(st[:, 2:3], st[:, 1:2], ACT.Identity, scale=st[:, 1:2]).then_inc(s_pre, 1)
            nc.scalar.activation(st[:, 3:4], prm[:, p_gamma:p_gamma + 1], ACT.Identity, scale=st[:, 1:2]).then_inc(s_pre, 1)
            act.wait_ge(s_zero, 4)

            def signs(wait_on, done):
                for n in range(G * YH):
                    yh, g = divmod(n, G)
                    act.wait_ge(wait_on, n + 1)
                    nc.scalar.activation(sg[:, g, 1 + yh * RH:1 + (yh + 1) * RH, 1:1 + W], rows(chunk(x1, g, yh)), ACT.Sign,
                                         bias=prm[:, p_move0:p_move0 + 1]).then_inc(done, 1)

            signs(s_x1, s_sg)
            act.wait_ge(s_flag, 1)
            beyond = act.value_load(flagi[0:1, 0:1], min_val=0, max_val=1)
            with act.If(beyond > 0):
                signs(s_gx, s_gs)
            act.end_ifs()
            nc.scalar.activation(st[:, 14:15], ones[:, 0:1], ACT.Sqrt)
            act.wait_ge(s_st, 3)
            nc.scalar.activation(st[:, 8:9], st[:, 7:8], ACT.Sqrt).then_inc(s_sd, 1)
            nc.scalar.activation(st[:, 15:16], st[:, 9:10], ACT.Identity, scale=-1.0).then_inc(s_shift, 1)
            act.wait_ge(s_k, 1)
            act.wait_ge(s_shift, 1)
            nc.scalar.activation(st[:, 12:13], st[:, 15:16], ACT.Identity, scale=st[:, 10:11], bias=st[:, 4:5]).then_inc(s_shift, 1)
            act.wait_ge(s_shift, 2)
            nc.scalar.activation(st[:, 13:14], st[:, 12:13], ACT.Identity, scale=prm[:, p_prelu:p_prelu + 1],
                                 bias=prm[:, p_move2:p_move2 + 1]).then_inc(s_shift, 1)
            act.wait_ge(s_shift, 3)
            for n in range(G * YH):
                yh, g = divmod(n, G)
                act.wait_ge(s_z, n + 1)
                nc.scalar.activation(chunk(zr, g, yh), chunk(zz, g, yh), ACT.Relu, bias=st[:, 12:13]).then_inc(s_r, 1)
                if n not in GPSIMD_LINES:
                    nc.scalar.activation(chunk(zq, g, yh), chunk(zz, g, yh), ACT.Identity, bias=st[:, 13:14],
                                         scale=prm[:, p_prelu:p_prelu + 1]).then_inc(s_q, 1)

        @block.gpsimd
        def _(pool):
            pool.memset(ones[:], 1.0).then_inc(s_zero, 1)
            pool.memset(vpad[:].rearrange("p g y a x -> p (g y a x)"), 0.0).then_inc(s_zero, 1)
            pool.memset(wcb[:].rearrange("p k c -> p (k c)"), 0.0).then_inc(s_zero, 1)
            pool.memset(sg[:].rearrange("p g y x -> p (g y x)"), 0.0).then_inc(s_zero, 1)

            def last_weight(m):
                if m not in GPSIMD_ROWS:
                    return
                yh, ky = divmod(m, TAPS)
                pool.wait_ge(s_ay, m + 1)
                pool.wait_ge(s_hat, 5 if yh == 0 else 12)
                if m >= 1:
                    pool.wait_ge(s_w, 2 * TAPS * m)
                pool.tensor_tensor(a[:, TAPS - 1, :], ay[:, yh, ky, :], hat[:, yh, TAPS - 1, :], ALU.mult).then_inc(s_ap, 1)

            last_weight(0)
            for m in range(TAPS * YH - 1):
                for j in range(2):
                    t = TAPS * m + 2 * j
                    pool.wait_ge(s_p, products_done(t + 1, G - 1))
                    if m >= 2:
                        pool.wait_ge(s_s4, m - 1)
                    pool.tensor_tensor(sum2[:, m % 2, j], prod[:, t % PR], prod[:, (t + 1) % PR], ALU.add).then_inc(s_s2, 1)
                last_weight(m + 1)
                if m == 1:
                    pool.wait_ge(s_rec, 2)
                    pool.tensor_tensor(grouped(prob[:, 1, :]), grouped(ex[:, 1, :]), spread_points(lrec[:, 1, :]),
                                       ALU.mult).then_inc(s_prob, 1)
                pool.wait_ge(s_s2, 2 * m + 2)
                if m >= 2:
                    pool.wait_ge(s_s8, m // 2)
                pool.tensor_tensor(sum4[:, m % 2], sum2[:, m % 2, 0], sum2[:, m % 2, 1], ALU.add).then_inc(s_s4, 1)
                if m % 2 and m // 2 in GPSIMD_PAIRS:
                    if m > 1:
                        pool.wait_ge(s_o, m // 2)
                    pool.wait_ge(s_s4, m + 1)
                    pool.tensor_tensor(sum8[:], sum4[:, 0], sum4[:, 1], ALU.add).then_inc(s_s8, 1)

            pool.wait_ge(s_shift, 3)
            for n in GPSIMD_LINES:
                yh, g = divmod(n, G)
                pool.wait_ge(s_z, n + 1)
                pool.tensor_scalar(chunk(zq, g, yh), chunk(zz, g, yh), prm[:, p_prelu:p_prelu + 1], st[:, 13:14], ALU.mult,
                                   ALU.add).then_inc(s_l, 1)

        @block.vector
        def _(dve):
            def positions(yh, d):
                dve.wait_ge(s_off, 2 * yh + d + 1)
                at = cst[:, c_pos:c_pos + W] if d == 0 else cst[:, c_pos + yh * RH:c_pos + (yh + 1) * RH]
                nc.vector.scalar_tensor_tensor(out=rows(u[:, d, yh, :]), in0=rows(ps_off[yh][d][:]),
                                               scalar=prm[:, p_off + d:p_off + d + 1], in1=along(at, d), op0=ALU.add,
                                               op1=ALU.add).then_inc(s_u, 1)

            def softmax_head(yh):
                dve.wait_ge(s_log, yh + 1)
                nc.vector.tensor_reduce(lmax[:, yh, :], grouped(ps_log[yh][:]), AX.X, ALU.max).then_inc(s_max, 1)
                dve.wait_ge(s_max, yh + 1)
                nc.vector.tensor_tensor(grouped(lsub[:, yh, :]), grouped(ps_log[yh][:]), spread_points(lmax[:, yh, :]),
                                        ALU.subtract).then_inc(s_sub, 1)

            def softmax_sum(yh):
                dve.wait_ge(s_exp, yh + 1)
                nc.vector.tensor_reduce(lsum[:, yh, :], grouped(ex[:, yh, :]), AX.X, ALU.add).then_inc(s_sum, 1)

            def softmax_recip(yh):
                dve.wait_ge(s_sum, yh + 1)
                nc.vector.reciprocal(lrec[:, yh, :], lsum[:, yh, :]).then_inc(s_rec, 1)

            def softmax_scale():
                dve.wait_ge(s_rec, 1)
                nc.vector.tensor_tensor(grouped(prob[:, 0, :]), grouped(ex[:, 0, :]), spread_points(lrec[:, 0, :]),
                                        ALU.mult).then_inc(s_prob, 1)

            def store_lower_values():
                dve.wait_ge(s_zero, 2)
                for g in range(G):
                    dve.wait_ge(s_v, G + g + 1)
                    nc.vector.tensor_scalar(values_of(g, 1), both_halves(ps_v[1][g][:]), prm[:, p_bv:p_bv + 1], None,
                                            ALU.add).then_inc(s_vlow, 1)

            def attend(yh, ky):
                dve.wait_ge(s_att, yh + 1)
                dve.wait_ge(s_hat, (2 if ky == 0 else 5 + ky) if yh == 0 else 13 + ky)
                nc.vector.tensor_tensor(ay[:, yh, ky, :], ps_att[yh][:], hat[:, yh, TAPS + ky, :], ALU.mult).then_inc(s_ay, 1)

            def weight(t):
                if is_gpsimds(t):
                    return
                yh, k = divmod(t, NT)
                ky, kx = divmod(k, TAPS)
                dve.wait_ge(s_ay, yh * TAPS + ky + 1)
                dve.wait_ge(s_hat, (1 if kx == 0 else 2 + kx) if yh == 0 else 9 + kx)
                if t >= TAPS:
                    dve.wait_ge(s_w, 2 * (t - TAPS + 1))
                nc.vector.tensor_tensor(a[:, t % TAPS, :], ay[:, yh, ky, :], hat[:, yh, kx, :], ALU.mult).then_inc(s_a, 1)

            def product(t):
                yh, k = divmod(t, NT)
                ky, kx = divmod(k, TAPS)
                if t == 0:
                    dve.wait_ge(s_vp, 2)
                    dve.wait_ge(s_vlow, 2)
                if t >= PR:
                    dve.wait_ge(s_s2, (t - PR) // 2 + 1)
                both = slice(0, G)
                for g in ([both] if t < NT * YH - 2 else [slice(g, g + 1) for g in range(G)]):
                    dve.wait_ge(s_w, 2 * t + g.stop)
                    nc.vector.tensor_tensor(by_half_row(prod[:, t % PR, g, :]), by_half_row(ps_w[t % 2][:, g, :]),
                                            v_window(g, yh, ky, kx), ALU.mult).then_inc(s_p, 1)

            def residual_of(yh, g, done):
                nc.vector.scalar_tensor_tensor(out=chunk(x1, g, yh), in0=ps_out[yh][g][:], scalar=prm[:, p_bo:p_bo + 1],
                                               in1=chunk(xs, g, yh), op0=ALU.add, op1=ALU.add).then_inc(done, 1)

            def residual(yh, done):
                for g in range(G):
                    residual_of(yh, g, done)

            def two_rows(j):
                dve.wait_ge(s_s4, 2 * j + 2)
                if j:
                    dve.wait_ge(s_o, j)
                nc.vector.tensor_tensor(sum8[:], sum4[:, 0], sum4[:, 1], ALU.add).then_inc(s_s8, 1)

            def last_pair(j):
                m = TAPS * YH - 1
                dve.wait_ge(s_s4, m - 1)
                for g in range(G):
                    t = TAPS * m + 2 * j
                    dve.wait_ge(s_p, products_done(t + 1, g))
                    nc.vector.tensor_tensor(sum2[:, 1, j, g, :], prod[:, t % PR, g, :], prod[:, (t + 1) % PR, g, :],
                                            ALU.add).then_inc(s_last, 1)

            def row_6_and_pair():
                dve.wait_ge(s_s4, TAPS * YH - 1)
                for g in range(G):
                    dve.wait_ge(s_last, g + 1)
                    nc.vector.tensor_tensor(sum4[:, 1, g, :], sum4[:, 0, g, :], sum2[:, 1, 0, g, :], ALU.add).then_inc(s_seven, 1)

            nc.vector.memset(top_ones[:], 0.0).then_inc(s_top, 1)
            dve.wait_ge(s_top, 1)
            nc.vector.memset(top_ones[0:1, :], 1.0).then_inc(s_top, 1)
            softmax_head(0)
            dve.wait_ge(s_cst, 16)
            dve.wait_ge(s_prm, 16)
            positions(0, 0)
            positions(0, 1)
            softmax_sum(0)
            softmax_recip(0)
            softmax_scale()
            attend(0, 0)
            weight(0)
            store_lower_values()
            weight(1)
            for t in range(NT * YH):
                if t % TAPS == 2 and t + 2 < NT * YH:
                    attend(*divmod((t + 2) // TAPS, TAPS))
                if t == 3:
                    softmax_head(1)
                if t == 4:
                    positions(1, 0)
                    positions(1, 1)
                if t == 5:
                    softmax_sum(1)
                if t == 6:
                    softmax_recip(1)
                if t == 17:
                    dve.wait_ge(s_fps, 1)
                    nc.vector.reduce_sum(flag[:, 0:1], ps_flag[0:1, 0:4], AX.X).then_inc(s_f1, 1)
                if t == 19:
                    dve.wait_ge(s_f1, 1)
                    nc.vector.tensor_scalar(flagi[:], flag[:, 0:1], 0.0, None, ALU.is_gt).then_inc(s_flag, 1)
                if t + 2 < NT * YH:
                    weight(t + 2)
                product(t)
                if t == 27:
                    dve.wait_ge(s_o, 2)
                    residual(0, s_x1)
                if t in (12, 20, 28) and (t - 12) // 8 not in GPSIMD_PAIRS:
                    two_rows((t - 12) // 8)
                if t == NT * YH - 2:
                    last_pair(0)
                    row_6_and_pair()
            last_pair(1)
            for g in range(G):
                dve.wait_ge(s_o, 4 + g)
                residual_of(1, g, s_x1)

            beyond = dve.value_load(flagi[0:1, 0:1], min_val=0, max_val=1)
            with dve.If(beyond > 0):
                dve.wait_ge(s_gt, 1)
                for yh in range(YH):
                    nc.vector.tensor_copy(gatt[:, yh * HALF:(yh + 1) * HALF], bank[yh][:]).then_inc(s_gd, 1)
                    for d in range(2):
                        at = cst[:, c_abs:c_abs + W] if d == 0 else cst[:, c_abs + yh * RH:c_abs + (yh + 1) * RH]
                        nc.vector.tensor_tensor(rows(gxy[:, d, yh * HALF:(yh + 1) * HALF]), rows(u[:, d, yh, :]), along(at, d),
                                                ALU.add).then_inc(s_gd, 1)
                nc.vector.memset(gacc[:].rearrange("p g n -> p (g n)"), 0.0).then_inc(s_gd, 1)

                def general_hat(axis, key, times, into, base, done):
                    dve.wait_ge(s_gd, base)
                    nc.vector.tensor_scalar(gt[:, 0, :], gxy[:, axis, :], cst[:, bass.ds(c_neg + key, 1)], 1.0, ALU.add,
                                            ALU.add).then_inc(s_gd, 1)
                    dve.wait_ge(s_gd, base + 1)
                    nc.vector.tensor_scalar(gt[:, 1, :], gt[:, 0, :], -1.0, 2.0, ALU.mult, ALU.add).then_inc(s_gd, 1)
                    dve.wait_ge(s_gd, base + 2)
                    nc.vector.tensor_tensor(gt[:, 0, :], gt[:, 0, :], gt[:, 1, :], ALU.min).then_inc(s_gd, 1)
                    dve.wait_ge(s_gd, base + 3)
                    nc.vector.scalar_tensor_tensor(out=into, in0=gt[:, 0, :], scalar=0.0, in1=times, op0=ALU.max,
                                                   op1=ALU.mult).then_inc(done, 1)

                SETUP, PER_Y, PER_X = 7, 4, 3 + G * YH
                with dve.Fori(0, H) as key_y:
                    at_y = SETUP + key_y * (PER_Y + PER_X * W)
                    general_hat(1, key_y, gatt, gay, at_y, s_gd)
                    for half in range(2):
                        with dve.Fori(0, HW) as key_x:
                            at_x = at_y + PER_Y + PER_X * HW * half + PER_X * key_x
                            general_hat(0, half * HW + key_x, gay, ga, at_x, s_ga)
                            dve.wait_ge(s_gw, W * key_y + half * HW + 1 + key_x)
                            for g in range(G):
                                first = (2 * -TAP0) * SEG + -TAP0 + half * (SEG - 1)
                                value = vpad[:, g].rearrange("p y a x -> p (y a x)")[
                                    :, bass.ds(key_y * (2 * SEG) + key_x + first, 1)]
                                for yh in range(YH):
                                    nc.vector.scalar_tensor_tensor(out=chunk(gacc, g, yh), in0=bank[4 + 2 * yh + g][:], scalar=value,
                                                                   in1=chunk(gacc, g, yh), op0=ALU.mult,
                                                                   op1=ALU.add).then_inc(s_gd, 1)
                dve.wait_ge(s_gd, SETUP + H * (PER_Y + PER_X * W))
                dve.sem_inc(s_gc, 1)
                dve.wait_ge(s_go, 1)
                dve.wait_ge(s_sg, 4)
                for yh in range(YH):
                    residual(yh, s_gx)
            dve.end_ifs()

            for n in range(G * YH):
                g, yh = divmod(n, YH)
                dve.wait_ge(s_y, n + 1)
                nc.vector.bn_stats(bns[:, n, :], ps_y[yh][g][:]).then_inc(s_bns, 1)
            dve.wait_ge(s_bns, G * YH)
            nc.vector.bn_aggr(mv[:], bns[:].rearrange("p n s -> p (n s)")).then_inc(s_mv, 1)
            dve.wait_ge(s_pair, 1)
            nc.vector.tensor_copy(st[:, 9:12], bank[4][:, 0:3]).then_inc(s_st, 1)
            dve.wait_ge(s_st, 1)
            dve.wait_ge(s_pre, 5)
            nc.vector.scalar_tensor_tensor(out=st[:, 6:7], in0=st[:, 11:12], scalar=st[:, 11:12], in1=st[:, 10:11], op0=ALU.mult,
                                           op1=ALU.add).then_inc(s_st, 1)
            dve.wait_ge(s_st, 2)
            nc.vector.tensor_scalar(st[:, 7:8], st[:, 6:7], st[:, 2:3], BN_EPS, ALU.mult, ALU.add).then_inc(s_st, 1)
            dve.wait_ge(s_sd, 1)
            nc.vector.reciprocal(st[:, 6:7], st[:, 8:9]).then_inc(s_st, 1)
            dve.wait_ge(s_st, 4)
            nc.vector.scalar_tensor_tensor(out=st[:, 8:9], in0=st[:, 6:7], scalar=st[:, 6:7], in1=st[:, 7:8], op0=ALU.mult,
                                           op1=ALU.mult).then_inc(s_st, 1)
            dve.wait_ge(s_st, 5)
            nc.vector.tensor_scalar(st[:, 11:12], st[:, 8:9], -0.5, 1.5, ALU.mult, ALU.add).then_inc(s_st, 1)
            dve.wait_ge(s_st, 6)
            nc.vector.scalar_tensor_tensor(out=st[:, 10:11], in0=st[:, 11:12], scalar=st[:, 6:7], in1=st[:, 3:4], op0=ALU.mult,
                                           op1=ALU.mult).then_inc(s_k, 1)
            def scaled(n):
                yh, g = divmod(n, G)
                if n == 0:
                    dve.wait_ge(s_k, 1)
                nc.vector.scalar_tensor_tensor(out=chunk(zz, g, yh), in0=ps_y[yh][g][:], scalar=st[:, 10:11], in1=chunk(x1, g, yh),
                                               op0=ALU.mult, op1=ALU.add).then_inc(s_z, 1)

            def prelu(n):
                yh, g = divmod(n, G)
                dve.wait_ge(s_r, n + 1)
                if n in GPSIMD_LINES:
                    dve.wait_ge(s_l, GPSIMD_LINES.index(n) + 1)
                else:
                    dve.wait_ge(s_q, n + 1 - len(GPSIMD_LINES))
                nc.vector.scalar_tensor_tensor(out=chunk(res, g, yh), in0=chunk(zr, g, yh), scalar=st[:, 5:6], in1=chunk(zq, g, yh),
                                               op0=ALU.mult, op1=ALU.add).then_inc(s_res, 1)

            scaled(0)
            scaled(1)
            scaled(2)
            scaled(3)
            prelu(0)
            prelu(1)
            prelu(2)
            prelu(3)


def kernel(**inputs):
    import concourse.bacc as _bacc
    from concourse.bass_utils import run_bass_kernel_spmd as _run

    def get(name):
        return np.ascontiguousarray(inputs[name])

    def blocks(w):
        out = np.zeros((P, w.shape[1] * PAIR), w.dtype)
        for i in range(PAIR):
            out[i * w.shape[0]:(i + 1) * w.shape[0], i * w.shape[1]:(i + 1) * w.shape[1]] = w
        return out

    w_off = get("L0_conv_W_off").reshape(C, HP, 2)
    w_proj = np.stack([blocks(w_off[:, :, 0]), blocks(w_off[:, :, 1]), blocks(get("L0_conv_W_attn"))], 1)
    conv_w = get("L1_conv_conv_w")
    params = [get(n).reshape(C) for n in ("L0_conv_b_value", "L0_conv_b_out", "L1_conv_move0_bias", "L1_conv_bn_gamma",
                                          "L1_conv_bn_beta", "L1_conv_move1_bias", "L1_conv_prelu_a", "L1_conv_move2_bias")]
    arrays = {
        "x": get("x"),
        "const": constants(),
        "w_in": np.concatenate([w_proj.reshape(P, -1), blocks(get("L0_conv_W_value"))], 1),
        "w_out": blocks(get("L0_conv_W_out")),
        "params": np.concatenate([np.tile(np.stack(params, 1), (PAIR, 1)), np.tile(get("L0_conv_b_off").reshape(HP, 2), (B, 1)),
                                  np.tile(get("L0_conv_b_attn").reshape(1, HP), (P, 1))], 1),
        "w_conv": np.tile(conv_w.transpose(1, 2, 3, 0).reshape(C, K * K * C), (PAIR, 1)),
        "w_abs": np.tile(conv_w.reshape(C, C * K * K), (PAIR, 1)),
    }
    arrays = {n + "_dram": np.ascontiguousarray(v) for n, v in arrays.items()}
    nc = _bacc.Bacc("TRN2", target_bir_lowering=False, num_devices=1)
    args = [nc.dram_tensor(n, v.shape, F32, kind="ExternalInput").ap() for n, v in arrays.items()]
    args.append(nc.dram_tensor("out_dram", (B, C, H, W), F32, kind="ExternalOutput").ap())
    deformable_attention_then_binary_conv(nc, *args)
    r = _run(nc, [arrays], core_ids=[0])
    return r.results[0]["out_dram"]
```
